# Optimizing a Trainium2 kernel written in Bass

```python
import numpy as np
import jax
import jax.numpy as jnp

def _softmax(x, axis=-1):
    return jax.nn.softmax(x, axis=axis)

def _gelu(x):
    return jax.nn.gelu(x, approximate=True)

def _silu(x):
    return jax.nn.silu(x)

def _sigmoid(x):
    return jax.nn.sigmoid(x)

def _layernorm(x, axis=-1, eps=1e-05):
    m = jnp.mean(x, axis=axis, keepdims=True)
    v = jnp.var(x, axis=axis, keepdims=True)
    return (x - m) / jnp.sqrt(v + eps)

def _scatter_add(tgt, idx, src, axis=0):
    return tgt.at[idx].add(src)

def _segment_sum(src, seg, n):
    return jax.ops.segment_sum(src, seg, n)
kernel_name = 'mk_decoder_postln_d1_seqx_r4_8301c0'

def setup_inputs(seed: int=0):
    np.random.seed(seed)
    _w = jnp.asarray

    def _rec_inputs():
        import jax
        import jax.numpy as jnp
        _rk = jax.random.key(seed)
        x = -0.0002928 + 1 * jax.random.normal(jax.random.fold_in(_rk, 1), (2, 1024, 256), jnp.float32)
        _lenS = 1024 - jax.random.randint(jax.random.fold_in(_rk, 7), (2,), 0, max(1, 1024 // 4) + 1, jnp.int32)
        _lenS2 = 77 - jax.random.randint(jax.random.fold_in(_rk, 8), (2,), 0, max(1, 77 // 4) + 1, jnp.int32)
        _ctx_1024P = jax.random.normal(jax.random.fold_in(_rk, 11), (2, 16, 256), jnp.float32)
        _ctx_1024c = jax.random.dirichlet(jax.random.fold_in(_rk, 511), 0.3 * jnp.ones((16,), jnp.float32), (2, 77))
        _ctx_1024t = jnp.einsum('bsk,bkd->bsd', _ctx_1024c, _ctx_1024P)
        _ctx_1024t = _ctx_1024t * jax.lax.rsqrt(jnp.mean(jnp.square(_ctx_1024t)) + 1e-12) * 0.953939
        ctx_1024 = -1.39393e-06 + 0.999914 * (_ctx_1024t + 0.3 * jax.random.normal(jax.random.fold_in(_rk, 611), (2, 77, 256), jnp.float32))
        _validS = jnp.arange(1024)[None, :] < _lenS[:, None]
        _validS2 = jnp.arange(77)[None, :] < _lenS2[:, None]
        _causal = jnp.tril(jnp.ones((1024, 1024), dtype=bool))
        mask_SxS2_bf1 = jnp.ones((1024, 77), dtype=bool)
        return (x, ctx_1024, mask_SxS2_bf1)
    x, ctx_1024, mask_SxS2_bf1 = _rec_inputs()

    def _L0_attn_setup():
        import jax, jax.numpy as jnp
        import numpy as np
        N_HEAD = 16
        ROPE_BASE = 10000.0

        def _rotate_half(t):
            d = t.shape[-1] // 2
            return jnp.concatenate([-t[..., d:], t[..., :d]], axis=-1)

        def _rope_cos_sin(T, D, dtype):
            half = D // 2
            theta = 1.0 / ROPE_BASE ** (jnp.arange(half, dtype=dtype) / half)
            pos = jnp.arange(T, dtype=dtype)
            freqs = pos[:, None] * theta[None, :]
            cos = jnp.repeat(jnp.cos(freqs), 2, axis=-1)
            sin = jnp.repeat(jnp.sin(freqs), 2, axis=-1)
            return (cos, sin)
        key = jax.random.key(seed)
        k1, k2, k3 = jax.random.split(key, 3)
        B, T, C = (2, 512, 256)
        x = jax.random.normal(k1, (B, T, C), dtype=jnp.float32)
        w_qkv = jax.random.normal(k2, (C, 3 * C), dtype=jnp.float32) * C ** (-0.5)
        w_proj = jax.random.normal(k3, (C, C), dtype=jnp.float32) * C ** (-0.5)
        return {'x': x, 'w_qkv': w_qkv, 'w_proj': w_proj}
    _L0_attn_all = _L0_attn_setup()
    _L0_attn_in = {k: v for k, v in _L0_attn_all.items() if k in ('w_qkv', 'w_proj')}
    del _L0_attn_all

    def _L0_xattn_setup():
        import jax, jax.numpy as jnp
        import numpy as np
        D_MODEL = 256
        NUM_HEADS = 16
        HEAD_DIM = D_MODEL // NUM_HEADS
        BATCH = 2
        SEQ = 512
        key = jax.random.key(seed)
        ks = jax.random.split(key, 12)
        s = 1.0 / np.sqrt(D_MODEL)
        inp = {'pre_query': jax.random.normal(ks[0], (BATCH, SEQ, D_MODEL), jnp.float32), 'pre_key': jax.random.normal(ks[1], (BATCH, SEQ, D_MODEL), jnp.float32), 'pre_value': jax.random.normal(ks[2], (BATCH, SEQ, D_MODEL), jnp.float32), 'mask': jnp.ones((SEQ, SEQ), dtype=bool), 'Wq': jax.random.normal(ks[3], (D_MODEL, D_MODEL), jnp.float32) * s, 'bq': jax.random.normal(ks[4], (D_MODEL,), jnp.float32) * s, 'Wk': jax.random.normal(ks[5], (D_MODEL, D_MODEL), jnp.float32) * s, 'bk': jax.random.normal(ks[6], (D_MODEL,), jnp.float32) * s, 'Wv': jax.random.normal(ks[7], (D_MODEL, D_MODEL), jnp.float32) * s, 'bv': jax.random.normal(ks[8], (D_MODEL,), jnp.float32) * s, 'Wo': jax.random.normal(ks[9], (D_MODEL, D_MODEL), jnp.float32) * s, 'bo': jax.random.normal(ks[10], (D_MODEL,), jnp.float32) * s}
        return inp
    _L0_xattn_all = _L0_xattn_setup()
    _L0_xattn_in = {k: v for k, v in _L0_xattn_all.items() if k in ('Wq', 'bq', 'Wk', 'bk', 'Wv', 'bv', 'Wo', 'bo')}
    del _L0_xattn_all

    def _L0_ffn_setup():
        import jax, jax.numpy as jnp
        import numpy as np
        D_IN, D_HID = (256, 1024)

        def _ternary(key, shape):
            return jax.random.randint(key, shape, -1, 2).astype(jnp.float32)

        def _tlin(x, w, s):
            return jnp.einsum('bsi,oi->bso', x, w) * s
        key = jax.random.key(seed)
        ks = jax.random.split(key, 12)
        inv = lambda fan: 1.0 / np.sqrt(fan).astype(np.float32)
        return {'x': jax.random.normal(ks[0], (4, 512, D_IN), dtype=jnp.float32), 'w1_w': _ternary(ks[1], (D_HID, D_IN)), 'w1_s': jax.random.uniform(ks[2], (D_HID,), dtype=jnp.float32) * inv(D_IN), 'w2_w': _ternary(ks[3], (D_HID, D_IN)), 'w2_s': jax.random.uniform(ks[4], (D_HID,), dtype=jnp.float32) * inv(D_IN), 'h1_w': _ternary(ks[5], (D_HID, D_HID)), 'h1_s': jax.random.uniform(ks[6], (D_HID,), dtype=jnp.float32) * inv(D_HID), 'h2_w': _ternary(ks[7], (D_HID, D_HID)), 'h2_s': jax.random.uniform(ks[8], (D_HID,), dtype=jnp.float32) * inv(D_HID), 'w3_w': _ternary(ks[9], (D_IN, D_HID)), 'w3_s': jax.random.uniform(ks[10], (D_IN,), dtype=jnp.float32) * inv(D_HID)}
    _L0_ffn_all = _L0_ffn_setup()
    _L0_ffn_in = {k: v for k, v in _L0_ffn_all.items() if k in ('w1_w', 'w1_s', 'w2_w', 'w2_s', 'h1_w', 'h1_s', 'h2_w', 'h2_s', 'w3_w', 'w3_s')}
    del _L0_ffn_all
    return {'x': x, 'ctx_1024': ctx_1024, 'mask_SxS2_bf1': mask_SxS2_bf1, 'L0_attn_w_qkv': _L0_attn_in['w_qkv'], 'L0_attn_w_proj': _L0_attn_in['w_proj'], 'L0_xattn_Wq': _L0_xattn_in['Wq'], 'L0_xattn_bq': _L0_xattn_in['bq'], 'L0_xattn_Wk': _L0_xattn_in['Wk'], 'L0_xattn_bk': _L0_xattn_in['bk'], 'L0_xattn_Wv': _L0_xattn_in['Wv'], 'L0_xattn_bv': _L0_xattn_in['bv'], 'L0_xattn_Wo': _L0_xattn_in['Wo'], 'L0_xattn_bo': _L0_xattn_in['bo'], 'L0_ffn_w1_w': _L0_ffn_in['w1_w'], 'L0_ffn_w1_s': _L0_ffn_in['w1_s'], 'L0_ffn_w2_w': _L0_ffn_in['w2_w'], 'L0_ffn_w2_s': _L0_ffn_in['w2_s'], 'L0_ffn_h1_w': _L0_ffn_in['h1_w'], 'L0_ffn_h1_s': _L0_ffn_in['h1_s'], 'L0_ffn_h2_w': _L0_ffn_in['h2_w'], 'L0_ffn_h2_s': _L0_ffn_in['h2_s'], 'L0_ffn_w3_w': _L0_ffn_in['w3_w'], 'L0_ffn_w3_s': _L0_ffn_in['w3_s']}

def reference(x, ctx_1024, mask_SxS2_bf1, L0_attn_w_qkv, L0_attn_w_proj, L0_xattn_Wq, L0_xattn_bq, L0_xattn_Wk, L0_xattn_bk, L0_xattn_Wv, L0_xattn_bv, L0_xattn_Wo, L0_xattn_bo, L0_ffn_w1_w, L0_ffn_w1_s, L0_ffn_w2_w, L0_ffn_w2_s, L0_ffn_h1_w, L0_ffn_h1_s, L0_ffn_h2_w, L0_ffn_h2_s, L0_ffn_w3_w, L0_ffn_w3_s):
    import jax
    import jax.numpy as jnp

    def _L0_attn_ref(x, w_qkv, w_proj):
        import jax, jax.numpy as jnp
        import numpy as np
        N_HEAD = 16
        ROPE_BASE = 10000.0

        def _rotate_half(t):
            d = t.shape[-1] // 2
            return jnp.concatenate([-t[..., d:], t[..., :d]], axis=-1)

        def _rope_cos_sin(T, D, dtype):
            half = D // 2
            theta = 1.0 / ROPE_BASE ** (jnp.arange(half, dtype=dtype) / half)
            pos = jnp.arange(T, dtype=dtype)
            freqs = pos[:, None] * theta[None, :]
            cos = jnp.repeat(jnp.cos(freqs), 2, axis=-1)
            sin = jnp.repeat(jnp.sin(freqs), 2, axis=-1)
            return (cos, sin)
        B, T, C = x.shape
        H = N_HEAD
        D = C // H
        scale = D ** (-0.5)
        qkv = x @ w_qkv
        q, k, v = jnp.split(qkv, 3, axis=-1)
        to_heads = lambda t: t.reshape(B, T, H, D).transpose(0, 2, 1, 3)
        q, k, v = (to_heads(q), to_heads(k), to_heads(v))
        cos, sin = _rope_cos_sin(T, D, x.dtype)
        q = q * cos + _rotate_half(q) * sin
        k = k * cos + _rotate_half(k) * sin
        att = jnp.einsum('bhtd,bhsd->bhts', q, k) * scale
        causal = jnp.tril(jnp.ones((T, T), dtype=bool))
        att = jnp.where(causal, att, jnp.finfo(att.dtype).min)
        att = jax.nn.softmax(att, axis=-1)
        y = jnp.einsum('bhts,bhsd->bhtd', att, v)
        y = y.transpose(0, 2, 1, 3).reshape(B, T, C)
        return y @ w_proj

    def _L0_xattn_ref(pre_query, pre_key, pre_value, mask, Wq, bq, Wk, bk, Wv, bv, Wo, bo):
        import jax, jax.numpy as jnp
        import numpy as np
        D_MODEL = 256
        NUM_HEADS = 16
        HEAD_DIM = D_MODEL // NUM_HEADS
        BATCH = 2
        SEQ = 512
        b = pre_query.shape[0]
        q = (pre_query @ Wq.T + bq).reshape(b, -1, NUM_HEADS, HEAD_DIM)
        k = (pre_key @ Wk.T + bk).reshape(b, -1, NUM_HEADS, HEAD_DIM)
        v = (pre_value @ Wv.T + bv).reshape(b, -1, NUM_HEADS, HEAD_DIM)
        scores = jnp.einsum('blhd,bLhd->bhlL', q, k) / jnp.sqrt(jnp.float32(HEAD_DIM))
        scores = jnp.where(mask, scores, jnp.float32(-jnp.inf))
        attn = jax.nn.softmax(scores, axis=-1)
        out = jnp.einsum('bhlL,bLhd->blhd', attn, v).reshape(b, -1, D_MODEL)
        return out @ Wo.T + bo

    def _L0_ffn_ref(x, w1_w, w1_s, w2_w, w2_s, h1_w, h1_s, h2_w, h2_s, w3_w, w3_s):
        import jax, jax.numpy as jnp
        import numpy as np
        D_IN, D_HID = (256, 1024)

        def _ternary(key, shape):
            return jax.random.randint(key, shape, -1, 2).astype(jnp.float32)

        def _tlin(x, w, s):
            return jnp.einsum('bsi,oi->bso', x, w) * s
        h = jax.nn.silu(_tlin(x, w1_w, w1_s)) * _tlin(x, w2_w, w2_s)
        h = jax.nn.gelu(_tlin(h, h1_w, h1_s), approximate=False)
        h = jax.nn.gelu(_tlin(h, h2_w, h2_s), approximate=False)
        return _tlin(h, w3_w, w3_s)
    x = _layernorm(x + _L0_attn_ref(x, L0_attn_w_qkv, L0_attn_w_proj), axis=-1)
    x = _layernorm(x + _L0_xattn_ref(x, ctx_1024, ctx_1024, mask_SxS2_bf1, L0_xattn_Wq, L0_xattn_bq, L0_xattn_Wk, L0_xattn_bk, L0_xattn_Wv, L0_xattn_bv, L0_xattn_Wo, L0_xattn_bo), axis=-1)
    x = _layernorm(x + _L0_ffn_ref(x, L0_ffn_w1_w, L0_ffn_w1_s, L0_ffn_w2_w, L0_ffn_w2_s, L0_ffn_h1_w, L0_ffn_h1_s, L0_ffn_h2_w, L0_ffn_h2_s, L0_ffn_w3_w, L0_ffn_w3_s), axis=-1)
    return x

_drawn_inputs = setup_inputs


def setup_inputs(seed=0):
    import zlib

    import numpy as np

    out = dict(_drawn_inputs(seed))
    spreads = {}
    factors = {'L0_xattn_bq': 4.145,
     'L0_xattn_bk': 8.0,
     'L0_ffn_w1_w': 8.0,
     'L0_ffn_w1_s': 8.0,
     'L0_ffn_w2_w': 8.0,
     'L0_ffn_w2_s': 8.0,
     'L0_ffn_h1_w': 8.0,
     'L0_ffn_h1_s': 8.0,
     'L0_ffn_h2_w': 8.0,
     'L0_ffn_h2_s': 8.0,
     'L0_ffn_w3_w': 8.0,
     'L0_ffn_w3_s': 8.0}
    for name, (base, spread) in spreads.items():
        noise = np.random.default_rng([zlib.crc32(name.encode()), seed]).standard_normal(out[name].shape)
        drawn = base * np.exp(spread * noise) if base else spread * noise
        out[name] = jnp.asarray(drawn.astype(out[name].dtype))
    for name, factor in factors.items():
        out[name] = (out[name] * factor).astype(out[name].dtype)
    return out
```

```python
from contextlib import ExitStack

import numpy as np

import concourse.bass as bass
from concourse import mybir

F32 = mybir.dt.float32
F32R = mybir.dt.float32r
BF16 = mybir.dt.bfloat16
U8 = mybir.dt.uint8
U32 = mybir.dt.uint32
I32 = mybir.dt.int32
ALU = mybir.AluOpType
ACT = mybir.ActivationFunctionType
AXX = mybir.AxisListType.X

P = 128
BATCH, T, D, H, HID, CTX = 2, 1024, 256, 16, 1024, 77
DH = D // H
NT = T // P
KD = D // P
KH = HID // P
NP = H // 2
NG = H // 4
SLOT = 64
MROW = 3 * DH
VW = DH + 1
VROW = H * VW + 16
CP = CTX + 1
CHUNK = 512
NC = T // CHUNK
SCALE = DH ** -0.5
EPS = 1e-5
NEG = -3.0e38
QKBUF = 5
FW = [KD * HID, KD * HID, KH * HID, KH * HID, KH * D]
FO = [sum(FW[:i]) for i in range(6)]
PIECES = 32
PW = FO[5] // PIECES
LOWBITS = 0xFFF

UNITS = [(hh, qt, half) for hh in range(2) for qt in range(NT) for half in range(1 + qt // 4)]
NU = len(UNITS)
STEPS = [(c, kb) for c in range(NC) for kb in range(4 * c + 4)]
NS = len(STEPS)
LAST = NG * NS


def pair_base(p):
    return NS * (p // 2) - (6 if p % 2 == 0 else 0)


def stage_step(p):
    return pair_base(p) - 13


def turn_step(p, i):
    return pair_base(p) - 12 + i


def max_step(p, u):
    return pair_base(p) - 8 + u // 4


def rows_step(p):
    return pair_base(p) - 2


def y_step(n):
    return NS * (n // 2) + (5 if n % 2 == 0 else 14)


FIRST_STEP = stage_step(0)
FINAL_STEP = y_step(2 * NG - 1)

ROUNDS = []
for _s in range(FIRST_STEP, FINAL_STEP + 1):
    ROUNDS += [("turn", p, i) for p in range(NP) for i in range(4) if turn_step(p, i) == _s]
    ROUNDS += [("rows", p, 0) for p in range(NP) if rows_step(p) == _s]
    ROUNDS += [("y", n, 0) for n in range(2 * NG) if y_step(n) == _s]
ROUND_AT = {r: n for n, r in enumerate(ROUNDS)}

XROUNDS = []
for _s in range(-6, 10):
    XROUNDS += [("turn", _s + 5, i) for i in range(2) if 0 <= _s + 5 < NP]
    XROUNDS += [("rows", _s + 3, 0)] if 0 <= _s + 3 < NP else []
    XROUNDS += [("y", _s - 2, 0)] if 0 <= _s - 2 < 2 * NG else []
XROUND_AT = {r: n for n, r in enumerate(XROUNDS)}
XUNITS = [(0, 3), (3, 3), (6, 2)]


def decoder_layer(nc, a):
    with ExitStack() as ctx:
        def sb(name, shape, dt):
            return ctx.enter_context(nc.sbuf_tensor(name, shape, dt))

        ffn_w = sb("ffn_w", [P, FO[5]], F32)
        w_qkv = sb("w_qkv", [P, KD, 3 * D], F32)
        w_proj = sb("w_proj", [P, KD, D], F32)
        w_q = sb("w_q", [P, KD, D], F32)
        w_o = sb("w_o", [P, KD, D], F32)
        bias_q = sb("bias_q", [P, D], F32)
        bias_k = sb("bias_k", [P, D], F32)
        bias_v = sb("bias_v", [P, D], F32)
        bias_o = sb("bias_o", [P, D], F32)
        scale_w3 = sb("scale_w3", [P, D], F32)
        scales = sb("scales", [P, 4, KH], F32)
        cos_t = sb("cos_t", [P, NT, DH], F32)
        sin_t = sb("sin_t", [P, NT, DH], F32)
        ident = sb("ident", [P, P], F32)
        ident_bf = sb("ident_bf", [P, P], BF16)
        causal_bf = sb("causal_bf", [P, P], BF16)
        ones = sb("ones", [P, 1], F32)
        minus_half = sb("minus_half", [P, 1], F32)
        xmask_bias = sb("xmask_bias", [P, NT, CP], BF16)
        xmask_t = sb("xmask_t", [P, T], BF16)
        kx_t = sb("kx_t", [P, NP, 2 * CP], F32R)
        vx = sb("vx", [P, VROW], F32)
        tok = sb("tok", [P, NT, D], F32)
        low_bits = sb("low_bits", [P, PW], U32)
        low_max = sb("low_max", [P, 1], F32)
        low_any = sb("low_any", [1, 1], I32)
        max_raw = sb("max_raw", [P, 2, 2, 2, NT], F32)
        max_split = sb("max_split", [P, 2, 2, 2, NT], F32R)
        max_rows = sb("max_rows", [32, 2, P], F32R)
        recip = sb("recip", [P, 16], F32)
        stats = sb("stats", [P, 2, 6], F32)
        mean_var = sb("mean_var", [P, 2, 2], F32)
        var_eps = sb("var_eps", [P, 2, 1], F32)
        rstd = sb("rstd", [P, 2, 1], F32)

        arena = (nc.sbuf_base + 31) // 32 * 32

        def at(name, shape, dt, offset):
            return nc.alloc_sbuf_tensor_at(name, shape, dt, offset=arena + offset)

        O_V, O_QK, O_STAGE, O_T = 0, 9216, 25600, 33792
        O_P = O_T + QKBUF * 8192
        O_Y = O_P + 16384
        v_sb = at("v_sb", [P, NT, VROW], F32, O_V)
        qk_tok = at("qk_tok", [P, 2, NP, NT, 2 * DH], F32, O_QK)
        x_tok = at("x_tok", [P, NT, D], F32, O_QK + 8192)
        stage = [at(f"stage_{n}", [P, NT * 2, 4, DH], F32R, O_STAGE + 4096 * i)
                 for i, n in enumerate("qk")]
        turned = [[at(f"{n}_t{b}", [P, T], F32R, O_T + 8192 * b + 4096 * i) for i, n in enumerate("qk")]
                  for b in range(QKBUF)]
        x_t = at("x_t", [P, KD, T], F32, O_T + 8192 * (QKBUF - 1))
        prob = [at(f"prob{i}", [P, CHUNK], F32, O_P + 2048 * i) for i in range(8)]
        y_sb = at("y_sb", [P, CHUNK], F32, O_Y)
        rope_a = [at(f"rope_a{i}", [P, CHUNK], F32, O_P + 2048 * i) for i in range(2)]
        rope_b = [at(f"rope_b{i}", [P, CHUNK], F32, O_P + 4096 + 2048 * i) for i in range(2)]
        w_kv = at("w_kv", [P, 2, KD, D], F32, O_P + 8192)
        ctx_t = at("ctx_t", [P, KD, CTX], F32, O_P + 12288)
        kx_tok = at("kx_tok", [P, NP, 2, DH], F32, O_P + 13312)
        y_t = [at(f"y_t{i}", [P, KD, P], F32, O_P + 1024 * i) for i in range(2)]
        x1_t = [at(f"x1_t{i}", [P, KD, P], F32, O_P + 2048 + 1024 * i) for i in range(2)]
        resid = [at(f"resid{i}", [P, D], F32, O_P + 4096 + 1024 * i) for i in range(2)]
        qx_t = [at(f"qx_t{i}", [P, T], F32R, O_T + 4096 * i) for i in range(NP)]
        xmask_u8 = at("xmask_u8", [P, NT, CTX], U8, O_T)
        xmask_t_u8 = at("xmask_t_u8", [CTX, T], U8, O_T + 4096)
        x_hl = [at(f"x_{n}", [P, KD, T], F32R, 8192 * i) for i, n in enumerate(("hi", "lo"))]
        hid = [[at(f"hid{b}_{n}", [P, KH, CHUNK], F32R, 25600 + 32768 * b + 16384 * i)
                for i, n in enumerate(("hi", "lo"))] for b in range(2)]
        act_raw = [at(f"act_raw{i}", [P, CHUNK], F32, 16384 + 2048 * i) for i in range(3)]
        silu_sb = at("silu_sb", [P, CHUNK], F32, 22528)
        resid_f = [at(f"resid_f{i}", [P, D], F32, O_Y + 1024 * i) for i in range(2)]

        bank = [ctx.enter_context(nc.psum_tensor(f"bank{i}", [P, CHUNK], F32)) for i in range(8)]

        def sem(name):
            return ctx.enter_context(nc.semaphore(name))

        w_in, mask_in, ffn_scratch_in, ffn_in = sem("w_in"), sem("mask_in"), sem("ffn_scratch_in"), sem("ffn_in")
        qkv_in = sem("qkv_in")
        set_pool, set_dve = sem("set_pool"), sem("set_dve")
        names = """next_in x_in filled qk_mm v_mm rope_mul rope_add v_evac
            ctx_mm ctx_add ctx_stage ctx_lo ctx_turn ctx_evac
            stage_hi stage_lo round_mm turn_evac rows_evac rows_in0 rows_in1 y_norm
            max_mm max_red max_op score_mm exp_done select_done av_done y_evac
            check_op flag_mm flag_set
            yt_mm yt_evac proj_mm ln_add ln_stats ln_aggr ln_eps ln_rstd ln_done xt_mm xt_evac
            q_mm q_add bo_add x_lo
            xstage_hi xstage_lo xround_mm xturn_evac xrows_evac xrows_in0 xrows_in1 xy_norm
            xmax_mm xmax_red xmax_op xscore_mm xexp_done xmask_dve xmask_pool xav_done xy_evac
            ffn_mm ffn_act ffn_gate act_hi act_lo ffn_out out_done""".split()
        S = {n: sem(n) for n in names}
        first, last = S[names[0]].num, S[names[-1]].num
        assert last - first == len(names) - 1

        def load_sequence(sp, b, arrived):
            sp.dma_start(x_t[:], a["x_t"][bass.ds(b, 1)].rearrange("o (k p) t -> p (o k) t", p=P)).then_inc(arrived, 16)
            sp.dma_start(ctx_t[:], a["ctx_t"][bass.ds(b, 1)].rearrange("o (k p) t -> p (o k) t", p=P)).then_inc(arrived, 16)
            for i, n in enumerate(("w_k", "w_v")):
                sp.dma_start(w_kv[:, i], a[n].rearrange("(k p) n -> p k n", p=P)).then_inc(arrived, 16)

        with nc.Block() as block:
            @block.sync
            def _(sp):
                sp.dma_start(xmask_u8[:], a["mask"].rearrange("(t p) k -> p t k", p=P)).then_inc(mask_in, 16)
                sp.dma_start(xmask_t_u8[:], a["mask_t"]).then_inc(mask_in, 16)
                load_sequence(sp, 0, qkv_in)
                sp.dma_start(w_qkv[:], a["w_qkv"].rearrange("(k p) n -> p k n", p=P)).then_inc(qkv_in, 16)
                sp.dma_start(cos_t[:], a["cos"]).then_inc(qkv_in, 16)
                sp.dma_start(sin_t[:], a["sin"]).then_inc(qkv_in, 16)

            @block.gpsimd
            def _(pool):
                pool.memset(ident[:], 0.0).then_inc(set_pool, 1)
                pool.memset(ident_bf[:], 0.0).then_inc(set_pool, 1)
                pool.memset(causal_bf[:], 0.0).then_inc(set_pool, 1)
                pool.memset(ones[:], 1.0).then_inc(set_pool, 1)
                pool.memset(minus_half[:], -0.5).then_inc(set_pool, 1)
                pool.memset(kx_t[:].bitcast(F32), 0.0).then_inc(set_pool, 1)
                pool.memset(vx[:], 1.0).then_inc(set_pool, 1)
                pool.wait_ge(set_pool, 7)
                for m in (ident, ident_bf):
                    pool.affine_select(out=m[:], in_=m[:], compare_op=ALU.not_equal, fill=1.0, base=0,
                                       pattern=[[-1, P]], channel_multiplier=1).then_inc(set_pool, 1)
                pool.affine_select(out=causal_bf[:], in_=causal_bf[:], compare_op=ALU.is_ge, fill=NEG, base=0,
                                   pattern=[[-1, P]], channel_multiplier=1).then_inc(set_pool, 1)

            @block.vector
            def _(dve):
                dve.memset(xmask_bias[:], 0.0).then_inc(set_dve, 1)
                dve.wait_ge(mask_in, 32)
                dve.wait_ge(set_dve, 1)
                dve.tensor_scalar(xmask_bias[:, :, 0:CTX], xmask_u8[:], 1.0, -NEG, ALU.subtract,
                                  ALU.mult).then_inc(set_dve, 1)
                dve.tensor_copy(xmask_t[0:CTX], xmask_t_u8[:]).then_inc(set_dve, 1)

        with nc.Fori(0, BATCH) as b:
            with nc.Block() as block:
                build_sequence(nc, block, b, dict(locals()), S)
            nc.all_engine_barrier(sems_to_clear=range(first, last + 1))


def build_sequence(nc, block, b, L, S):
    a = L["a"]
    bank, ident, tok, turned, stage, prob = (L[k] for k in ("bank", "ident", "tok", "turned", "stage", "prob"))
    x_t, qk_tok, x_tok, v_sb, y_sb, kx_t, vx = (L[k] for k in ("x_t", "qk_tok", "x_tok", "v_sb", "y_sb", "kx_t", "vx"))
    w_kv, ctx_t, kx_tok = L["w_kv"], L["ctx_t"], L["kx_tok"]
    max_raw, max_split, max_rows, recip = L["max_raw"], L["max_split"], L["max_rows"], L["recip"]
    y_t, x1_t, resid, resid_f, qx_t = L["y_t"], L["x1_t"], L["resid"], L["resid_f"], L["qx_t"]
    x_hl, hid, act_raw, silu_sb, ffn_w, scales = (L[k] for k in ("x_hl", "hid", "act_raw", "silu_sb", "ffn_w", "scales"))
    stats, mean_var, var_eps, rstd = L["stats"], L["mean_var"], L["var_eps"], L["rstd"]
    low_bits, low_max, low_any = L["low_bits"], L["low_max"], L["low_any"]
    qkv_in, w_in, ffn_in, ffn_scratch_in, set_pool, set_dve = (L[k] for k in ("qkv_in", "w_in", "ffn_in", "ffn_scratch_in", "set_pool", "set_dve"))
    A_BANK, S_BANK, Y_BANK, R_BANK = bank[0:2], bank[2:6], bank[6], bank[7]

    def qkt(p, which):
        return turned[p % QKBUF][which]

    def unit_bank(n):
        return bank[n % 6] if n < 2 * NU else A_BANK[n % 2]

    def v_window(v, h):
        return v[:, VW * h:VW * h + 32]

    def consumer(rounds, n, prefix):
        kind = rounds[n][0]
        count = sum(r[0] == kind for r in rounds[:n + 1])
        name = {"turn": "turn_evac", "rows": "rows_evac", "y": "y_norm"}[kind]
        return S[prefix + name], count * (2 if kind == "y" else 1)

    def w_view(i, dtype):
        n = D if i == 4 else HID
        v = ffn_w[:, FO[i]:FO[i + 1]]
        return (v if dtype is F32 else v.bitcast(dtype)).rearrange("p (k n) -> p k n", n=n)

    @block.sync
    def _(sp):
        with sp.If(b == 0):
            for dst, name in ((L["bias_k"], "bk"), (L["bias_v"], "bv"), (L["bias_q"], "bq"), (L["bias_o"], "bo"), (L["scale_w3"], "s3")):
                sp.dma_start(dst[:], a[name].rearrange("(o n) -> o n", o=1).to_broadcast([P, D])).then_inc(w_in, 16)
            for name in ("w_proj", "w_q", "w_o"):
                sp.dma_start(L[name][:], a[name].rearrange("(k p) n -> p k n", p=P)).then_inc(w_in, 16)
            sp.dma_start(scales[:], a["scales"]).then_inc(w_in, 16)
            for name in ("w1", "w2", "h1", "h2", "w3"):
                sp.dma_start(a["scratch_" + name], a[name]).then_inc(ffn_scratch_in, 16)
            sp.wait_ge(ffn_scratch_in, 16 * 5)
            for i, name in enumerate(("w1", "w2", "h1", "h2", "w3")):
                sp.dma_start(w_view(i, F32), a["scratch_" + name].rearrange("(k p) n -> p k n", p=P)).then_inc(ffn_in, 16)
        for p in range(NP):
            if p == NP - 1:
                sp.wait_ge(S["stage_hi"], 2 * NP)
                sp.wait_ge(S["stage_lo"], 2 * NP)
                sp.dma_start(x_tok[:], a["x"][bass.ds(b, 1)].rearrange("o (t p) n -> p (o t) n", p=P)).then_inc(S["x_in"], 16)
            sp.wait_ge(S["rows_evac"], p + 1)
            sp.wait_ge(S["turn_evac"], 4 * p + 4)
            sp.wait_ge(S["max_mm"], NU * (p + 1))
            for hh in range(2):
                for r in range(2):
                    q0 = 16 * hh + 8 * r
                    row = SLOT * hh + MROW + r
                    sp.dma_start(qkt(p, 0)[row:row + 1, :].bitcast(F32), max_rows[q0:q0 + 8, p % 2, :].bitcast(F32)).then_inc(S[f"rows_in{p % 2}"], 16)
        for p in range(NP):
            sp.wait_ge(S["xrows_evac"], p + 1)
            sp.wait_ge(S["xturn_evac"], 2 * p + 2)
            sp.wait_ge(S["xmax_mm"], 3 * (p + 1))
            for hh in range(2):
                for r in range(2):
                    q0 = 16 * hh + 8 * r
                    row = SLOT * hh + MROW + r
                    sp.dma_start(qx_t[p][row:row + 1, :].bitcast(F32), max_rows[q0:q0 + 8, p % 2, :].bitcast(F32)).then_inc(S[f"xrows_in{p % 2}"], 16)
        with sp.If(b < BATCH - 1):
            sp.wait_ge(S["ffn_mm"], 36 * NC - 4)
            L["load_sequence"](sp, nc.s_assert_within(b + 1, 1, BATCH - 1, skip_runtime_bounds_check_because="the branch is taken below the last sequence alone"), S["next_in"])
            sp.wait_ge(S["next_in"], 16 * 4)
        for t in range(NT):
            sp.wait_ge(S["ln_done"], 2 * NT + t + 1)
            sp.dma_start(a["out"][bass.ds(b, 1)].rearrange("o (t p) n -> p (o t) n", p=P)[:, t, :], tok[:, t, :]
                         ).then_inc(S["out_done"], 16)
        sp.wait_ge(S["out_done"], 16 * NT)

    @block.tensor
    def _(pe):
        mm = pe.matmul

        def project_qkv(t):
            if t >= 2:
                pe.wait_ge(S["rope_mul"], 3 * (t - 1))
                pe.wait_ge(S["v_evac"], t - 1)
            qk, v = bank[2 + t % 2], bank[4 + t % 2]
            xs = x_t[:, :, P * t:P * (t + 1)]
            for k in range(KD):
                i = mm(qk[:], xs[:, k], L["w_qkv"][:, k, 0:2 * D], start=k == 0, stop=k == KD - 1)
            i.then_inc(S["qk_mm"], 1)
            for k in range(KD):
                i = mm(v[:, 0:D], xs[:, k], L["w_qkv"][:, k, 2 * D:3 * D], start=k == 0, stop=k == KD - 1)
            i.then_inc(S["v_mm"], 1)

        def project_ctx():
            for i in range(2):
                for k in range(KD):
                    m = mm(bank[i][0:CTX, 0:D], ctx_t[:, k], w_kv[:, i, k], start=k == 0, stop=k == KD - 1)
                m.then_inc(S["ctx_mm"], 1)

        def turn_ctx(j):
            if j == 0:
                pe.wait_ge(S["ctx_stage"], 3)
            for q in range(4):
                m = pe.transpose(bank[j][:, P * q:P * q + CTX], ctx_pair(4 * j + q), ident[0:CTX, 0:CTX])
            m.then_inc(S["ctx_turn"], 1)

        def ctx_pair(p):
            return stage[1][0:CTX, 2 * p:2 * p + 2].rearrange("p h a e -> p (h a e)").bitcast(F32)

        def use_round(rounds, at, key, prefix):
            n = at[key]
            if n:
                pe.wait_ge(*consumer(rounds, n - 1, prefix))
            return n

        def turn(p, i):
            if i == 0:
                pe.wait_ge(S["stage_hi"], 2 * (p + 1))
                pe.wait_ge(S["stage_lo"], 2 * (p + 1))
            use_round(ROUNDS, ROUND_AT, ("turn", p, i), "")
            st = stage[i // 2][:].bitcast(F32)
            for q in range(4):
                t = 4 * (i % 2) + q
                m = pe.transpose(R_BANK[:, P * q:P * (q + 1)], st[:, 2 * t:2 * t + 2].rearrange("p h a e -> p (h a e)"), ident[:])
            m.then_inc(S["round_mm"], 1)

        def max_unit(p, u):
            n = NU * p + u
            if u == 0:
                pe.wait_ge(S["turn_evac"], 4 * (p + 1))
            ahead = 6 if p < 2 else 2
            if n >= ahead:
                pe.wait_ge(S["max_red"], n - ahead + 1)
            hh, qt, half = UNITS[u]
            k0, k1 = CHUNK * half, min(CHUNK * (half + 1), P * (qt + 1))
            out, r = unit_bank(n), slice(SLOT * hh, SLOT * (hh + 1))
            diagonal = k1 == P * (qt + 1)
            m = mm(out[:, 0:k1 - k0], qkt(p, 0)[r, P * qt:P * (qt + 1)], qkt(p, 1)[r, k0:k1], start=True, stop=not diagonal)
            if diagonal:
                m = mm(out[:, k1 - k0 - P:k1 - k0], L["ident_bf"][:], L["causal_bf"][:], start=False, stop=True)
            m.then_inc(S["max_mm"], 1)

        def rows(p):
            pe.wait_ge(S["max_op"], 3 * (p + 1))
            use_round(ROUNDS, ROUND_AT, ("rows", p, 0), "")
            src = max_split[:, p % 2].rearrange("p h r t -> p (h r t)").bitcast(F32)
            pe.transpose(R_BANK[0:32, 0:P], src, ident[:]).then_inc(S["round_mm"], 1)

        def y_turn(n):
            pe.wait_ge(S["y_evac"], n + 1)
            use_round(ROUNDS, ROUND_AT, ("y", n, 0), "")
            for i in range(4):
                m = pe.transpose(R_BANK[:, P * i:P * (i + 1)], y_sb[:, P * i:P * (i + 1)], ident[:])
            m.then_inc(S["round_mm"], 1)

        def score(s, j):
            g, (c, kb) = s // NS, STEPS[s % NS]
            if s % NS == 0 and j == 0:
                pe.wait_ge(S["rows_in0"], 64 * (g + 1))
                pe.wait_ge(S["rows_in1"], 64 * (g + 1))
            q0 = max(0, kb - 4 * c) * P
            if s:
                pe.wait_ge(S["exp_done"], 4 * (s - 1) + j + 1)
            elif j == 0:
                pe.wait_ge(S["max_red"], 2 * NU)
            p, r = 2 * g + j // 2, slice(SLOT * (j % 2), SLOT * (j % 2 + 1))
            mm(S_BANK[j][:, 0:CHUNK - q0], qkt(p, 1)[r, P * kb:P * (kb + 1)],
               qkt(p, 0)[r, CHUNK * c + q0:CHUNK * (c + 1)], start=True, stop=True).then_inc(S["score_mm"], 1)

        def values(s):
            g, (c, kb) = s // NS, STEPS[s % NS]
            pe.wait_ge(S["exp_done"], 4 * s + 4)
            diag = max(0, kb - 4 * c) if kb >= 4 * c else 0
            if kb >= 4 * c:
                pe.wait_ge(S["select_done"], 4 * (1 + sum(STEPS[i % NS][1] >= 4 * STEPS[i % NS][0] for i in range(s))))
            n = 2 * g + c
            if kb == 0 and n:
                pe.wait_ge(S["y_evac"], n)
            q0 = diag * P
            for j in range(4):
                m = mm(Y_BANK[32 * j:32 * (j + 1), q0:CHUNK], v_window(v_sb[:, kb], 4 * g + j),
                       prob[4 * (s % 2) + j][:, 0:CHUNK - q0], start=kb == 0, stop=kb == 4 * c + 3)
            m.then_inc(S["av_done"], 1)

        def y_to_features(k, t):
            n = NT * k + t
            if t == 0:
                pe.wait_ge(S["xy_norm" if k else "y_norm"], 4 * NG)
            if t < 2:
                pe.wait_ge(S["xmax_red" if k else "max_red"], (3 if k else NU) * NP)
            else:
                pe.wait_ge(S["yt_evac"], n - 1)
            for i in range(KD):
                m = pe.transpose(bank[t % 2][:, P * i:P * (i + 1)], tok[:, t, P * i:P * (i + 1)], ident[:])
            m.then_inc(S["yt_mm"], 1)

        def project_out(k, t):
            n = NT * k + t
            pe.wait_ge(S["yt_evac"], n + 1)
            if t < 2:
                pe.wait_ge(S["xexp_done" if k else "exp_done"], 32 if k else 4 * LAST)
            else:
                pe.wait_ge(S["ln_add"], n - 1)
            for i in range(KD):
                m = mm(bank[2 + t % 2][:, 0:D], y_t[t % 2][:, i], L["w_o" if k else "w_proj"][:, i], start=i == 0, stop=i == KD - 1)
            m.then_inc(S["proj_mm"], 1)

        def x_to_features(k, t):
            n = NT * k + t
            pe.wait_ge(S["ln_done"], n + 1)
            if t >= 2:
                pe.wait_ge(S["xt_evac"], n - 1)
                if k:
                    pe.wait_ge(S["x_lo"], t - 1)
            for i in range(KD):
                m = pe.transpose(bank[4 + t % 2][:, P * i:P * (i + 1)], tok[:, t, P * i:P * (i + 1)], ident[:])
            m.then_inc(S["xt_mm"], 1)

        def project_q(t):
            pe.wait_ge(S["xt_evac"], t + 1)
            if t >= 2:
                pe.wait_ge(S["q_add"], t - 1)
            for i in range(KD):
                m = mm(bank[6 + t % 2][:, 0:D], x1_t[t % 2][:, i], L["w_q"][:, i], start=i == 0, stop=i == KD - 1)
            m.then_inc(S["q_mm"], 1)

        def x_turn(p, i):
            if i == 0:
                pe.wait_ge(S["xstage_lo"], p + 1)
                pe.wait_ge(S["xstage_hi"], p + 1)
                if p == 0:
                    pe.wait_ge(S["q_add"], NT)
            use_round(XROUNDS, XROUND_AT, ("turn", p, i), "x")
            st = stage[0][:].bitcast(F32)
            for q in range(4):
                t = 4 * i + q
                m = pe.transpose(R_BANK[:, P * q:P * (q + 1)], st[:, 2 * t:2 * t + 2].rearrange("p h a e -> p (h a e)"), ident[:])
            m.then_inc(S["xround_mm"], 1)

        def x_max(p, u):
            n = 3 * p + u
            if u == 0:
                pe.wait_ge(S["xturn_evac"], 2 * (p + 1))
            if n >= 2:
                pe.wait_ge(S["xmax_red"], n - 1)
            else:
                pe.wait_ge(S["yt_evac"], NT)
            t0, nt = XUNITS[u]
            out = A_BANK[n % 2][:, 0:2 * CP * nt]
            mask = L["xmask_bias"][:, t0:t0 + nt].unsqueeze(2).to_broadcast([P, nt, 2, CP])
            mm(out.rearrange("p (t h k) -> p t h k", h=2, k=CP), L["ident_bf"][:], mask, start=True, stop=False)
            for i in range(nt):
                t = t0 + i
                m = mm(out[:, 2 * CP * i:2 * CP * (i + 1)], qx_t[p][:, P * t:P * (t + 1)], kx_t[:, p], start=False, stop=i == nt - 1)
            m.then_inc(S["xmax_mm"], 1)

        def x_rows(p):
            pe.wait_ge(S["xmax_op"], 2 * (p + 1))
            use_round(XROUNDS, XROUND_AT, ("rows", p, 0), "x")
            src = max_split[:, p % 2].rearrange("p h r t -> p (h r t)").bitcast(F32)
            pe.transpose(R_BANK[0:32, 0:P], src, ident[:]).then_inc(S["xround_mm"], 1)

        def x_scores(s):
            g, c = s // 2, s % 2
            if c == 0:
                pe.wait_ge(S["xrows_in0"], 64 * (g + 1))
                pe.wait_ge(S["xrows_in1"], 64 * (g + 1))
            if s == 0:
                pe.wait_ge(S["ln_add"], NT)
                pe.wait_ge(S["xt_evac"], NT)
            for j in range(4):
                if s:
                    pe.wait_ge(S["xexp_done"], 4 * (s - 1) + j + 1)
                p, hh = 2 * g + j // 2, j % 2
                r = slice(SLOT * hh, SLOT * (hh + 1))
                mm(S_BANK[j][0:CTX, :], kx_t[r, p, CP * hh:CP * hh + CTX],
                   qx_t[p][r, CHUNK * c:CHUNK * (c + 1)], start=True, stop=True).then_inc(S["xscore_mm"], 1)

        def x_values(s):
            g = s // 2
            pe.wait_ge(S["xmask_dve"], 2 * s + 2)
            pe.wait_ge(S["xmask_pool"], 2 * s + 2)
            if s:
                pe.wait_ge(S["xy_evac"], s)
            for j in range(4):
                m = mm(Y_BANK[32 * j:32 * (j + 1), :], v_window(vx[0:CTX], 4 * g + j),
                       prob[4 * (s % 2) + j][0:CTX, :], start=True, stop=True)
            m.then_inc(S["xav_done"], 1)

        def x_y_turn(n):
            pe.wait_ge(S["xy_evac"], n + 1)
            use_round(XROUNDS, XROUND_AT, ("y", n, 0), "x")
            for i in range(4):
                m = pe.transpose(R_BANK[:, P * i:P * (i + 1)], y_sb[:, P * i:P * (i + 1)], ident[:])
            m.then_inc(S["xround_mm"], 1)

        def group_free(c, n):
            q = 36 * c + n - 8
            if q < 0:
                return
            c, n = q // 36, q % 36
            if n < 16 and n % 2 == 0:
                pe.wait_ge(S["ffn_act"], 24 * c + n // 2 + 1)
            elif n < 16:
                pe.wait_ge(S["ffn_gate"], 8 * c + n // 2 + 1)
            elif n < 32:
                pe.wait_ge(S["ffn_act"], 24 * c + n - 16 + 8 + 1)
            else:
                pe.wait_ge(S["ffn_out"], 4 * c + n - 32 + 1)

        def ffn(exact):
            dt = F32R if exact else F32

            def view(ap):
                return ap if exact else ap.bitcast(F32)

            for c in range(NC):
                tokens = slice(CHUNK * c, CHUNK * (c + 1))
                for m in range(KH):
                    for i in range(2):
                        n = 2 * m + i
                        group_free(c, n)
                        out = bank[(36 * c + n) % 8]
                        for k in range(KD):
                            for part in range(2):
                                o = mm(out[:], w_view(i, dt)[:, k, P * m:P * (m + 1)], view(x_hl[part][:, k, tokens]),
                                       start=k + part == 0, stop=(k, part) == (KD - 1, 1))
                        o.then_inc(S["ffn_mm"], 1)
                for layer in range(2):
                    src = hid[layer]
                    for m in range(KH):
                        n = 16 + 8 * layer + m
                        group_free(c, n)
                        out = bank[(36 * c + n) % 8]
                        for k in range(KH):
                            if m == 0:
                                pe.wait_ge(S["act_hi"], 24 * c + 8 * layer + k + 1)
                                pe.wait_ge(S["act_lo"], 24 * c + 8 * layer + k + 1)
                            for part in range(2):
                                o = mm(out[:], w_view(2 + layer, dt)[:, k, P * m:P * (m + 1)], view(src[part][:, k]),
                                       start=k + part == 0, stop=(k, part) == (KH - 1, 1))
                        o.then_inc(S["ffn_mm"], 1)
                for i in range(4):
                    n = 32 + i
                    group_free(c, n)
                    out = bank[(36 * c + n) % 8]
                    for k in range(KH):
                        if i == 0:
                            pe.wait_ge(S["act_hi"], 24 * c + 16 + k + 1)
                            pe.wait_ge(S["act_lo"], 24 * c + 16 + k + 1)
                        for part in range(2):
                            o = mm(out[:, 0:D], view(hid[0][part][:, k, P * i:P * (i + 1)]), w_view(4, dt)[:, k],
                                   start=k + part == 0, stop=(k, part) == (KH - 1, 1))
                    o.then_inc(S["ffn_mm"], 1)

        pe.wait_ge(set_pool, 10)
        pe.wait_ge(set_dve, 3)
        pe.wait_ge(qkv_in, 16 * 7)
        for t in range(NT):
            project_qkv(t)
            if t == 1:
                project_ctx()
            if t == 5:
                turn_ctx(0)
            if t == 6:
                turn_ctx(1)
        pe.wait_ge(S["v_evac"], NT)
        pe.wait_ge(S["rope_mul"], 3 * NT)
        pe.wait_ge(S["ctx_evac"], 4)
        for s in range(FIRST_STEP, FINAL_STEP + 1):
            units = [(p, u) for p in range(NP) for u in range(NU) if max_step(p, u) == s]
            for j in range(4):
                if 0 <= s < LAST:
                    score(s, j)
                for unit in units[j:j + 1]:
                    max_unit(*unit)
                for kind, i, k in ROUNDS:
                    if kind == "turn" and j == 1 and turn_step(i, k) == s:
                        turn(i, k)
                    if kind == "rows" and j == 1 and rows_step(i) == s:
                        rows(i)
                    if kind == "y" and j == 3 and y_step(i) == s:
                        y_turn(i)
            if 0 <= s - 1 < LAST:
                values(s - 1)
        pe.wait_ge(w_in, 16 * 9)
        for s in range(NT + 4):
            if s < NT:
                y_to_features(0, s)
            if 0 <= s - 1 < NT:
                project_out(0, s - 1)
            if 0 <= s - 3 < NT:
                x_to_features(0, s - 3)
            if 0 <= s - 4 < NT:
                project_q(s - 4)
        with pe.If(b == 0):
            pe.wait_ge(S["check_op"], PIECES + 3)
            pe.wait_ge(S["q_add"], NT)
            mm(Y_BANK[0:1, 0:1], low_max[:], L["ones"][:], start=True, stop=True).then_inc(S["flag_mm"], 1)
            pe.wait_ge(S["flag_set"], 1)
        for s in range(-6, 10):
            if 0 <= s + 5 < NP:
                x_turn(s + 5, 0)
            if 0 <= s < 2 * NG:
                x_scores(s)
            if 0 <= s + 5 < NP:
                x_turn(s + 5, 1)
            if 0 <= s + 4 < NP:
                for u in range(3):
                    x_max(s + 4, u)
            if 0 <= s + 3 < NP:
                x_rows(s + 3)
            if 0 <= s - 1 < 2 * NG:
                x_values(s - 1)
            if 0 <= s - 2 < 2 * NG:
                x_y_turn(s - 2)
        for s in range(NT + 3):
            if s < NT:
                y_to_features(1, s)
            if 0 <= s - 1 < NT:
                project_out(1, s - 1)
            if 0 <= s - 3 < NT:
                x_to_features(1, s - 3)
        pe.wait_ge(ffn_in, 16 * 5)
        pe.wait_ge(S["xt_evac"], 2 * NT)
        pe.wait_ge(S["x_lo"], NT)
        with pe.register("low_bits_any") as found:
            pe.reg_load(found, low_any[0:1, 0:1])
            with pe.If_eq(found, 0):
                ffn(exact=True)
            with pe.If_ne(found, 0):
                ffn(exact=False)

    @block.scalar
    def _(act):
        def evac_round(rounds, at, key, prefix, out, src, name, dt=None):
            act.wait_ge(S[prefix + "round_mm"], at[key] + 1)
            act.activation(out, src, ACT.Copy).then_inc(S[prefix + name], 1)

        def v_evac(t):
            act.wait_ge(S["v_mm"], t + 1)
            if t == 0:
                act.wait_ge(S["filled"], 3)
            act.activation(v_sb[:, t, 0:H * VW].rearrange("p (h w) -> p h w", w=VW)[:, :, 0:DH],
                           bank[4 + t % 2][:, 0:D].rearrange("p (h e) -> p h e", e=DH), ACT.Copy).then_inc(S["v_evac"], 1)

        def ctx_evac(j):
            act.wait_ge(S["ctx_turn"], j + 1)
            for hh in range(2):
                r = slice(SLOT * hh, SLOT * (hh + 1))
                act.activation(kx_t[r, 4 * j:4 * j + 4, CP * hh:CP * hh + CTX],
                               bank[j][r].rearrange("p (q k) -> p q k", k=P)[:, :, 0:CTX], ACT.Copy).then_inc(S["ctx_evac"], 1)

        def turn_evac(p, i):
            if p >= QKBUF:
                act.wait_ge(S["score_mm"], 4 * NS * ((p - QKBUF) // 2 + 1))
            c = CHUNK * (i % 2)
            evac_round(ROUNDS, ROUND_AT, ("turn", p, i), "", qkt(p, i // 2)[:, c:c + CHUNK], R_BANK[:], "turn_evac")

        def rows_evac(p):
            if p >= 2:
                act.wait_ge(S[f"rows_in{p % 2}"], 64 * (p // 2))
            evac_round(ROUNDS, ROUND_AT, ("rows", p, 0), "", max_rows[:, p % 2], R_BANK[0:32, 0:P], "rows_evac")

        def exps(s, heads):
            g, (c, kb) = s // NS, STEPS[s % NS]
            n = CHUNK - max(0, kb - 4 * c) * P
            if s >= 2 and heads[0] == 0:
                act.wait_ge(S["av_done"], s - 1)
            for j in heads:
                act.wait_ge(S["score_mm"], 4 * s + j + 1)
                act.activation(prob[4 * (s % 2) + j][:, 0:n], S_BANK[j][:, 0:n], ACT.Exp, scale=SCALE).then_inc(S["exp_done"], 1)

        def yt_evac(k, t):
            n = NT * k + t
            act.wait_ge(S["yt_mm"], n + 1)
            if t >= 2:
                act.wait_ge(S["proj_mm"], n - 1)
            act.activation(y_t[t % 2][:], bank[t % 2][:, 0:D].rearrange("p (k n) -> p k n", k=KD), ACT.Copy).then_inc(S["yt_evac"], 1)

        def xt_evac(k, t):
            act.wait_ge(S["xt_mm"], NT * k + t + 1)
            if k == 0 and t >= 2:
                act.wait_ge(S["q_mm"], t - 1)
            out = x_hl[0][:, :, P * t:P * (t + 1)] if k else x1_t[t % 2][:]
            act.activation(out, bank[4 + t % 2][:, 0:D].rearrange("p (k n) -> p k n", k=KD), ACT.Copy).then_inc(S["xt_evac"], 1)

        def x_exps(s):
            if s >= 2:
                act.wait_ge(S["xav_done"], s - 1)
            for j in range(4):
                act.wait_ge(S["xscore_mm"], 4 * s + j + 1)
                act.activation(prob[4 * (s % 2) + j][0:CTX], S_BANK[j][0:CTX, :], ACT.Exp, scale=SCALE).then_inc(S["xexp_done"], 1)

        act.wait_ge(set_pool, 10)
        for t in range(NT):
            v_evac(t)
            if t == 5:
                ctx_evac(0)
            if t == 6:
                ctx_evac(1)
        act.wait_ge(S["rope_add"], NT)
        for s in range(FIRST_STEP, FINAL_STEP + 1):
            if 0 <= s < LAST:
                exps(s, (0, 1))
            for kind, i, j in ROUNDS:
                if kind == "turn" and turn_step(i, j) == s:
                    turn_evac(i, j)
                if kind == "rows" and rows_step(i) == s:
                    rows_evac(i)
            if 0 <= s < LAST:
                exps(s, (2, 3))
        act.wait_ge(S["av_done"], LAST)
        for s in range(NT + 4):
            if s < NT:
                yt_evac(0, s)
            if 0 <= s - 3 < NT:
                xt_evac(0, s - 3)
        act.wait_ge(S["q_mm"], NT)
        act.wait_ge(S["ln_done"], NT)
        for s in range(-6, 10):
            if 0 <= s + 5 < NP:
                evac_round(XROUNDS, XROUND_AT, ("turn", s + 5, 0), "x", qx_t[s + 5][:, 0:CHUNK], R_BANK[:], "turn_evac")
            if 0 <= s < 2 * NG:
                x_exps(s)
            if 0 <= s + 5 < NP:
                evac_round(XROUNDS, XROUND_AT, ("turn", s + 5, 1), "x", qx_t[s + 5][:, CHUNK:T], R_BANK[:], "turn_evac")
            if 0 <= s + 3 < NP:
                p = s + 3
                if p >= 2:
                    act.wait_ge(S[f"xrows_in{p % 2}"], 64 * (p // 2))
                else:
                    act.wait_ge(S[f"rows_in{p % 2}"], 64 * NG)
                evac_round(XROUNDS, XROUND_AT, ("rows", p, 0), "x", max_rows[:, p % 2], R_BANK[0:32, 0:P], "rows_evac")
        act.wait_ge(S["xav_done"], 2 * NG)
        act.wait_ge(S["xstage_lo"], NP)
        act.wait_ge(S["xstage_hi"], NP)
        for s in range(NT + 3):
            if s < NT:
                yt_evac(1, s)
            if 0 <= s - 3 < NT:
                xt_evac(1, s - 3)
        act.wait_ge(S["ln_done"], 2 * NT)
        for c in range(NC):
            for m in range(KH):
                act.wait_ge(S["ffn_mm"], 36 * c + 2 * m + 1)
                if c or m:
                    act.wait_ge(S["ffn_gate"], 8 * c + m)
                act.activation(silu_sb[:], bank[(36 * c + 2 * m) % 8][:], ACT.Silu, scale=scales[:, 0, m:m + 1]).then_inc(S["ffn_act"], 1)
            for layer in range(2):
                for m in range(KH):
                    r = 24 * c + 8 + 8 * layer + m
                    n = 36 * c + 16 + 8 * layer + m
                    act.wait_ge(S["ffn_mm"], n + 1)
                    act.wait_ge(S["act_hi"], r - 2)
                    act.wait_ge(S["act_lo"], r - 2)
                    act.activation(act_raw[r % 3][:], bank[n % 8][:], ACT.Gelu, scale=scales[:, 2 + layer, m:m + 1]).then_inc(S["ffn_act"], 1)

    @block.vector
    def _(dve):
        tt = dve.tensor_tensor

        def rope(t):
            dve.wait_ge(S["qk_mm"], t + 1)
            if t >= 2:
                dve.wait_ge(S["rope_add"], t - 1)
            x = bank[2 + t % 2][:].rearrange("p (h e) -> p h e", e=DH)
            ra, rb = (r[t % 2][:].rearrange("p (h e) -> p h e", e=DH) for r in (L["rope_a"], L["rope_b"]))
            cos, sin = (L[n][:, t].unsqueeze(1).to_broadcast([P, 2 * H, DH]) for n in ("cos_t", "sin_t"))
            h = DH // 2
            tt(ra, x, cos, ALU.mult).then_inc(S["rope_mul"], 1)
            tt(rb[:, :, 0:h], x[:, :, h:DH], sin[:, :, 0:h], ALU.mult).then_inc(S["rope_mul"], 1)
            tt(rb[:, :, h:DH], x[:, :, 0:h], sin[:, :, h:DH], ALU.mult).then_inc(S["rope_mul"], 1)

        def ctx_add():
            dve.wait_ge(S["ctx_mm"], 1)
            tt(kx_tok[0:CTX].rearrange("p a h e -> p (a h e)"), bank[0][0:CTX, 0:D], L["bias_k"][0:CTX], ALU.add).then_inc(S["ctx_add"], 1)
            dve.wait_ge(S["ctx_mm"], 2)
            tt(vx[0:CTX, 0:H * VW].rearrange("p (h w) -> p h w", w=VW)[:, :, 0:DH],
               bank[1][0:CTX, 0:D].rearrange("p (h e) -> p h e", e=DH),
               L["bias_v"][0:CTX].rearrange("p (h e) -> p h e", e=DH), ALU.add).then_inc(S["ctx_add"], 1)
            dve.wait_ge(S["ctx_add"], 1)
            dve.wait_ge(S["filled"], 3)
            k = kx_tok[0:CTX].rearrange("p a h e -> p (a h) e")
            st = stage[1][0:CTX]
            for i, part in enumerate((0, 2)):
                dve.tensor_copy(st[:, :, part], k).then_inc(S["ctx_stage"], 1)
            dve.wait_ge(S["ctx_stage"], 2)
            tt(st[:, :, 1], k, st[:, :, 0].bitcast(F32), ALU.subtract).then_inc(S["ctx_stage"], 1)

        def stage_hi(p):
            if p == 0:
                dve.wait_ge(S["rope_add"], NT)
                dve.wait_ge(S["ctx_turn"], 2)
            else:
                dve.wait_ge(S["round_mm"], ROUND_AT[("turn", p - 1, 3)] + 1)
            for i in range(2):
                src = qk_tok[:, i, p].rearrange("p t (h e) -> p (t h) e", h=2).unsqueeze(2).to_broadcast([P, 2 * NT, 2, DH])
                dst = stage[i][:, :, 0:3 if i else 2:2 if i else 1]
                dve.tensor_copy(dst, src).then_inc(S["stage_hi"], 1)

        def reduce_unit(p, u):
            n = NU * p + u
            hh, qt, half = UNITS[u]
            if u == 0 and p >= 2:
                dve.wait_ge(S["max_op"], 3 * (p - 1))
            dve.wait_ge(S["max_mm"], n + 1)
            k = min(CHUNK, P * (qt + 1) - CHUNK * half)
            dve.tensor_reduce(max_raw[:, p % 2, hh, half, qt:qt + 1], unit_bank(n)[:, 0:k], AXX, ALU.max).then_inc(S["max_red"], 1)

        def split_max(p):
            raw, sp = max_raw[:, p % 2], max_split[:, p % 2]
            dve.wait_ge(S["max_red"], NU * (p + 1))
            tt(raw[:, :, 0, 4:NT], raw[:, :, 0, 4:NT], raw[:, :, 1, 4:NT], ALU.max).then_inc(S["max_op"], 1)
            dve.wait_ge(S["max_op"], 3 * p + 1)
            if p >= 2:
                dve.wait_ge(S["round_mm"], ROUND_AT[("rows", p - 2, 0)] + 1)
            dve.tensor_scalar(sp[:, :, 0], raw[:, :, 0], -1.0, None, ALU.mult).then_inc(S["max_op"], 1)
            dve.wait_ge(S["max_op"], 3 * p + 2)
            dve.scalar_tensor_tensor(out=sp[:, :, 1], in0=raw[:, :, 0], scalar=-1.0, in1=sp[:, :, 0].bitcast(F32),
                                     op0=ALU.mult, op1=ALU.subtract).then_inc(S["max_op"], 1)

        def y_evac(n, x=""):
            if n:
                at, rounds = (XROUND_AT, "xround_mm") if x else (ROUND_AT, "round_mm")
                dve.wait_ge(S[rounds], at[("y", n - 1, 0)] + 1)
            dve.wait_ge(S[x + "av_done"], n + 1 if x else NS * (n // 2) + (4 if n % 2 == 0 else NS))
            dve.tensor_copy(y_sb[:], Y_BANK[:]).then_inc(S[x + "y_evac"], 1)

        def y_norm(n, x=""):
            at = XROUND_AT if x else ROUND_AT
            dve.wait_ge(S[x + "round_mm"], at[("y", n, 0)] + 1)
            g, c = n // 2, n % 2
            y = R_BANK[:].rearrange("p (i j e) -> p i j e", i=4, j=4)
            rc = recip[:].rearrange("p (i j o) -> p i j o", i=4, j=4)
            if n:
                dve.wait_ge(S[x + "y_norm"], 2 * n)
            dve.reciprocal(rc, y[:, :, :, DH:DH + 1]).then_inc(S[x + "y_norm"], 1)
            dve.wait_ge(S[x + "y_norm"], 2 * n + 1)
            out = tok[:, 4 * c:4 * c + 4, 4 * DH * g:4 * DH * (g + 1)].rearrange("p i (j e) -> p i j e", e=DH)
            tt(out, y[:, :, :, 0:DH], rc.to_broadcast([P, 4, 4, DH]), ALU.mult).then_inc(S[x + "y_norm"], 1)

        def check_piece(n):
            with dve.If(b == 0):
              if n == 0:
                dve.wait_ge(ffn_in, 16 * 5)
              dve.wait_ge(S["check_op"], n + 1)
              tt(low_bits[:], low_bits[:], ffn_w[:, PW * n:PW * (n + 1)].bitcast(U32), ALU.bitwise_or).then_inc(S["check_op"], 1)

        def ln_stats(n, xr):
            dve.wait_ge(S["ln_add"], n + 1)
            dve.bn_stats(stats[:, n % 2], xr).then_inc(S["ln_stats"], 1)
            dve.wait_ge(S["ln_stats"], n + 1)
            dve.bn_aggr(mean_var[:, n % 2], stats[:, n % 2]).then_inc(S["ln_aggr"], 1)

        def ln_finish(n, xr):
            dve.wait_ge(S["ln_rstd"], n + 1)
            dve.wait_ge(S["ln_aggr"], n + 1)
            dve.tensor_scalar(tok[:, n % NT], xr, mean_var[:, n % 2, 0:1], rstd[:, n % 2], ALU.subtract, ALU.mult).then_inc(S["ln_done"], 1)

        def residual(k, t):
            n = NT * k + t
            dve.wait_ge(S["proj_mm"], n + 1)
            if t >= 2:
                dve.wait_ge(S["ln_done"], n - 1)
            if k:
                dve.wait_ge(S["bo_add"], t + 1)
            tt(resid[t % 2][:], bank[2 + t % 2][:, 0:D], x_tok[:, t], ALU.add).then_inc(S["ln_add"], 1)
            ln_stats(n, resid[t % 2][:])

        def q_add(t):
            dve.wait_ge(S["q_mm"], t + 1)
            tt(qk_tok[:, 0, :, t], bank[6 + t % 2][:, 0:D].rearrange("p (a e) -> p a e", a=NP),
               L["bias_q"][:].rearrange("p (a e) -> p a e", a=NP), ALU.add).then_inc(S["q_add"], 1)

        def x_stage_hi(p):
            if p:
                dve.wait_ge(S["xround_mm"], XROUND_AT[("turn", p - 1, 1)] + 1)
            else:
                dve.wait_ge(S["q_add"], NT)
            src = qk_tok[:, 0, p].rearrange("p t (h e) -> p (t h) e", h=2).unsqueeze(2).to_broadcast([P, 2 * NT, 2, DH])
            dve.tensor_copy(stage[0][:, :, 0:2], src).then_inc(S["xstage_hi"], 1)

        def x_reduce(p, u):
            n = 3 * p + u
            if u == 0:
                if p >= 2:
                    dve.wait_ge(S["xmax_op"], 2 * (p - 1))
            dve.wait_ge(S["xmax_mm"], n + 1)
            t0, nt = XUNITS[u]
            src = A_BANK[n % 2][:, 0:2 * CP * nt].rearrange("p (t h k) -> p t h k", h=2, k=CP)[:, :, :, 0:CTX]
            dst = max_raw[:, p % 2, :, 0, t0:t0 + nt].rearrange("p h t -> p t h")
            dve.tensor_reduce(dst, src, AXX, ALU.max).then_inc(S["xmax_red"], 1)

        def x_split_max(p):
            raw, sp = max_raw[:, p % 2], max_split[:, p % 2]
            dve.wait_ge(S["xmax_red"], 3 * (p + 1))
            if p >= 2:
                dve.wait_ge(S["xround_mm"], XROUND_AT[("rows", p - 2, 0)] + 1)
            dve.tensor_scalar(sp[:, :, 0], raw[:, :, 0], -1.0, None, ALU.mult).then_inc(S["xmax_op"], 1)
            dve.wait_ge(S["xmax_op"], 2 * p + 1)
            dve.scalar_tensor_tensor(out=sp[:, :, 1], in0=raw[:, :, 0], scalar=-1.0, in1=sp[:, :, 0].bitcast(F32),
                                     op0=ALU.mult, op1=ALU.subtract).then_inc(S["xmax_op"], 1)

        def x_mask(s):
            for j in range(2):
                dve.wait_ge(S["xexp_done"], 4 * s + j + 1)
                pr = prob[4 * (s % 2) + j][0:CTX]
                tt(pr, pr, L["xmask_t"][0:CTX, CHUNK * (s % 2):CHUNK * (s % 2 + 1)], ALU.mult).then_inc(S["xmask_dve"], 1)

        def hi_part(r, dst):
            dve.tensor_copy(dst, act_raw[r % 3][:]).then_inc(S["act_hi"], 1)

        dve.wait_ge(qkv_in, 16 * 7)
        dve.wait_ge(set_pool, 10)
        for t in range(NT):
            rope(t)
            if t == 2:
                dve.wait_ge(w_in, 16 * 9)
                ctx_add()
        for s in range(FIRST_STEP, FINAL_STEP + 1):
            for p in range(NP):
                if stage_step(p) == s:
                    stage_hi(p)
            for p in range(NP):
                for u in range(NU):
                    if max_step(p, u) == s:
                        reduce_unit(p, u)
                if max_step(p, NU - 1) == s:
                    split_max(p)
            if LAST - PIECES <= s < LAST:
                check_piece(s - (LAST - PIECES))
            for n in range(2 * NG):
                if y_step(n) == s:
                    y_norm(n)
                if NS * (n // 2) + (4 if n % 2 == 0 else NS) == s:
                    y_evac(n)
        with dve.If(b == 0):
            dve.wait_ge(S["check_op"], PIECES + 1)
            dve.tensor_scalar(low_bits[:], low_bits[:], LOWBITS, None, ALU.bitwise_and).then_inc(S["check_op"], 1)
            dve.wait_ge(S["check_op"], PIECES + 2)
            dve.tensor_reduce(low_max[:], low_bits[:], AXX, ALU.max).then_inc(S["check_op"], 1)
        dve.wait_ge(S["x_in"], 16)
        dve.wait_ge(S["av_done"], LAST)
        for s in range(NT + 5):
            if s < NT:
                residual(0, s)
            if 0 <= s - 1 < NT:
                ln_finish(s - 1, resid[(s - 1) % 2][:])
            if 0 <= s - 3 < NT:
                q_add(s - 3)
        with dve.If(b == 0):
            dve.wait_ge(S["flag_mm"], 1)
            dve.tensor_copy(low_any[:], Y_BANK[0:1, 0:1]).then_inc(S["flag_set"], 1)
        for s in range(-6, 10):
            if 0 <= s + 6 < NP:
                x_stage_hi(s + 6)
            if 0 <= s + 4 < NP:
                for u in range(3):
                    x_reduce(s + 4, u)
                x_split_max(s + 4)
            if 0 <= s < 2 * NG:
                x_mask(s)
            if 0 <= s - 1 < 2 * NG:
                y_evac(s - 1, "x")
            if 0 <= s - 2 < 2 * NG:
                y_norm(s - 2, "x")
        dve.wait_ge(S["xav_done"], 2 * NG)
        for s in range(NT + 5):
            if s < NT:
                residual(1, s)
            if 0 <= s - 1 < NT:
                ln_finish(NT + s - 1, resid[(s - 1) % 2][:])
            if 0 <= s - 4 < NT:
                t = s - 4
                dve.wait_ge(S["xt_evac"], NT + t + 1)
                sl = slice(P * t, P * (t + 1))
                tt(x_hl[1][:, :, sl], bank[4 + t % 2][:, 0:D].rearrange("p (k n) -> p k n", k=KD),
                   x_hl[0][:, :, sl].bitcast(F32), ALU.subtract).then_inc(S["x_lo"], 1)
        for c in range(NC):
            for m in range(KH):
                r, n = 24 * c + m, 36 * c + 2 * m + 1
                dve.wait_ge(S["ffn_mm"], n + 1)
                dve.wait_ge(S["ffn_act"], 24 * c + m + 1)
                if r >= 3:
                    dve.wait_ge(S["act_hi"], r - 2)
                    dve.wait_ge(S["act_lo"], r - 2)
                dve.scalar_tensor_tensor(out=act_raw[r % 3][:], in0=bank[n % 8][:], scalar=scales[:, 1, m:m + 1],
                                         in1=silu_sb[:], op0=ALU.mult, op1=ALU.mult).then_inc(S["ffn_gate"], 1)
                dve.wait_ge(S["ffn_gate"], 8 * c + m + 1)
                hi_part(r, hid[0][0][:, m])
            for layer in range(2):
                for m in range(KH):
                    r = 24 * c + 8 + 8 * layer + m
                    dve.wait_ge(S["ffn_act"], r + 1)
                    hi_part(r, hid[1 - layer][0][:, m])
            for i in range(5):
                if i < 4:
                    t = 4 * c + i
                    n = 2 * NT + t
                    xr = resid_f[t % 2]
                    dve.wait_ge(S["ffn_mm"], 36 * c + 32 + i + 1)
                    if t >= 2:
                        dve.wait_ge(S["ln_done"], n - 1)
                    tt(xr[:], bank[(36 * c + 32 + i) % 8][:, 0:D], L["scale_w3"][:], ALU.mult).then_inc(S["ffn_out"], 1)
                    dve.wait_ge(S["ffn_out"], t + 1)
                    tt(xr[:], xr[:], tok[:, t], ALU.add).then_inc(S["ln_add"], 1)
                    ln_stats(n, xr[:])
                if i >= 1:
                    t = 4 * c + i - 1
                    ln_finish(2 * NT + t, resid_f[t % 2][:])

    @block.gpsimd
    def _(pool):
        pt = pool.tensor_tensor
        pool.memset(v_sb[:], 1.0).then_inc(S["filled"], 1)
        pool.memset(stage[0][:, :, 3].bitcast(F32), 0.0).then_inc(S["filled"], 1)
        pool.memset(stage[1][:, :, 3].bitcast(F32), 1.0).then_inc(S["filled"], 1)
        pool.memset(low_bits[:], 0).then_inc(S["check_op"], 1)

        def rope_add(t):
            pool.wait_ge(S["rope_mul"], 3 * (t + 1))
            out = qk_tok[:, :, :, t].rearrange("p a b e -> p (a b) e")
            ra, rb = (r[t % 2][:].rearrange("p (a e) -> p a e", a=2 * NP) for r in (L["rope_a"], L["rope_b"]))
            pt(out, ra, rb, ALU.add).then_inc(S["rope_add"], 1)

        def stage_lo(p):
            for i in range(2):
                pool.wait_ge(S["stage_hi"], 2 * p + i + 1)
                src = qk_tok[:, i, p].rearrange("p t (h e) -> p (t h) e", h=2)
                pt(stage[i][:, :, 1 if i else 2], src, stage[i][:, :, 0].bitcast(F32), ALU.subtract).then_inc(S["stage_lo"], 1)

        def select(s):
            c, kb = STEPS[s % NS]
            if kb < 4 * c:
                return
            for j in range(4):
                pool.wait_ge(S["exp_done"], 4 * s + j + 1)
                pr = prob[4 * (s % 2) + j][:, 0:P]
                pool.affine_select(out=pr, in_=pr, compare_op=ALU.is_ge, fill=0.0, base=0,
                                   pattern=[[1, P]], channel_multiplier=-1).then_inc(S["select_done"], 1)

        def ln_rstd(n):
            pool.wait_ge(S["ln_aggr"], n + 1)
            if n >= 2:
                pool.wait_ge(S["ln_done"], n - 1)
            pool.tensor_scalar(var_eps[:, n % 2], mean_var[:, n % 2, 1:2], EPS, None, ALU.add).then_inc(S["ln_eps"], 1)
            pool.wait_ge(S["ln_eps"], n + 1)
            pt(rstd[:, n % 2], var_eps[:, n % 2], L["minus_half"][:], ALU.pow).then_inc(S["ln_rstd"], 1)

        for t in range(NT):
            rope_add(t)
        for s in range(FIRST_STEP, FINAL_STEP + 1):
            for p in range(NP):
                if stage_step(p) == s:
                    stage_lo(p)
            if 0 <= s < LAST:
                select(s)
        pool.wait_ge(w_in, 16 * 9)
        for s in range(NT + 1):
            if s < NT:
                ln_rstd(s)
            if s >= 1:
                pool.wait_ge(S["ln_done"], s)
                pt(x_tok[:, s - 1], tok[:, s - 1], L["bias_o"][:], ALU.add).then_inc(S["bo_add"], 1)
        for s in range(-6, 10):
            if 0 <= s + 6 < NP:
                p = s + 6
                pool.wait_ge(S["xstage_hi"], p + 1)
                src = qk_tok[:, 0, p].rearrange("p t (h e) -> p (t h) e", h=2)
                pt(stage[0][:, :, 2], src, stage[0][:, :, 0].bitcast(F32), ALU.subtract).then_inc(S["xstage_lo"], 1)
            if 0 <= s < 2 * NG:
                for j in range(2, 4):
                    pool.wait_ge(S["xexp_done"], 4 * s + j + 1)
                    pr = prob[4 * (s % 2) + j][0:CTX]
                    pt(pr, pr, L["xmask_t"][0:CTX, CHUNK * (s % 2):CHUNK * (s % 2 + 1)], ALU.mult).then_inc(S["xmask_pool"], 1)
        for t in range(NT):
            ln_rstd(NT + t)
        for c in range(NC):
            for r in range(24):
                n = 24 * c + r
                dst = hid[0 if r < 8 or r >= 16 else 1]
                pool.wait_ge(S["act_hi"], n + 1)
                pt(dst[1][:, r % 8], act_raw[n % 3][:], dst[0][:, r % 8].bitcast(F32), ALU.subtract).then_inc(S["act_lo"], 1)
            for i in range(4):
                ln_rstd(2 * NT + 4 * c + i)


def rope_tables():
    half = DH // 2
    theta = (np.float32(1.0) / np.float32(10000.0) ** (np.arange(half, dtype=np.float32) / np.float32(half))).astype(np.float32)
    freqs = (np.arange(T, dtype=np.float32)[:, None] * theta[None, :]).astype(np.float32)
    cos = np.repeat(np.cos(freqs), 2, axis=-1).astype(np.float32)
    sin = np.repeat(np.sin(freqs), 2, axis=-1).astype(np.float32)
    sin[:, :half] *= -1
    return [np.ascontiguousarray(t.reshape(NT, P, DH).transpose(1, 0, 2)) for t in (cos, sin)]


def kernel(**inputs):
    import concourse.bacc as bacc
    from concourse.bass_utils import run_bass_kernel_spmd

    g = {k: np.asarray(v) for k, v in inputs.items()}
    cos, sin = rope_tables()
    mask = g["mask_SxS2_bf1"].view(np.uint8)
    arrays = {
        "x": g["x"], "x_t": g["x"].transpose(0, 2, 1), "ctx_t": g["ctx_1024"].transpose(0, 2, 1),
        "mask": mask, "mask_t": mask.T,
        "w_qkv": g["L0_attn_w_qkv"], "w_proj": g["L0_attn_w_proj"],
        "w_q": g["L0_xattn_Wq"].T, "w_k": g["L0_xattn_Wk"].T, "w_v": g["L0_xattn_Wv"].T, "w_o": g["L0_xattn_Wo"].T,
        "bq": g["L0_xattn_bq"], "bk": g["L0_xattn_bk"], "bv": g["L0_xattn_bv"], "bo": g["L0_xattn_bo"],
        "w1": g["L0_ffn_w1_w"].T, "w2": g["L0_ffn_w2_w"].T, "h1": g["L0_ffn_h1_w"].T, "h2": g["L0_ffn_h2_w"].T,
        "w3": g["L0_ffn_w3_w"].T, "s3": g["L0_ffn_w3_s"],
        "scales": np.stack([g[f"L0_ffn_{n}_s"].reshape(KH, P).T for n in ("w1", "w2", "h1", "h2")], axis=1),
        "cos": cos, "sin": sin,
    }
    nc = bacc.Bacc("TRN2", target_bir_lowering=False, num_devices=1, dynamic_dma_scratch_size=1024)
    aps, feeds = {}, {}
    for name, arr in arrays.items():
        arr = np.ascontiguousarray(arr)
        feeds["in_" + name] = arr
        aps[name] = nc.dram_tensor("in_" + name, arr.shape, mybir.dt.from_np(arr.dtype), kind="ExternalInput").ap()
    for name in ("w1", "w2", "h1", "h2", "w3"):
        aps["scratch_" + name] = nc.dram_tensor("scratch_" + name, arrays[name].shape, F32).ap()
    aps["out"] = nc.dram_tensor("out_0", (BATCH, T, D), F32, kind="ExternalOutput").ap()
    decoder_layer(nc, aps)
    r = run_bass_kernel_spmd(nc, [feeds], core_ids=[0])
    return r.results[0]["out_0"]
```

```python
from contextlib import ExitStack

import numpy as np

import concourse.bass as bass
from concourse import mybir

F32 = mybir.dt.float32
F32R = mybir.dt.float32r
BF16 = mybir.dt.bfloat16
U8 = mybir.dt.uint8
U32 = mybir.dt.uint32
I32 = mybir.dt.int32
ALU = mybir.AluOpType
ACT = mybir.ActivationFunctionType
AXX = mybir.AxisListType.X

P = 128
BATCH, T, D, H, HID, CTX = 2, 1024, 256, 16, 1024, 77
DH = D // H
NT = T // P
KD = D // P
KH = HID // P
NP = H // 2
NG = H // 4
SLOT = 64
MROW = 3 * DH
VW = DH + 1
VROW = H * VW + 16
CP = CTX + 1
CHUNK = 512
NC = T // CHUNK
SCALE = DH ** -0.5
EPS = 1e-5
NEG = -3.0e38
QKBUF = 5
FW = [KD * HID, KD * HID, KH * HID, KH * HID, KH * D]
FO = [sum(FW[:i]) for i in range(6)]
PIECES = 16
PW = FO[5] // PIECES
LOWBITS = 0xFFF

UNITS = [(hh, qt, half) for qt in range(NT) for half in range(1 + qt // 4) for hh in (1, 0)]
NU = len(UNITS)
STEPS = [(g, c, kb) for g in range(NG) for c in range(NC) for kb in range(4 * c + 4)]
LAST = len(STEPS)
NS = LAST // NG
CHUNKS = [(g, c) for g, c, kb in STEPS if kb == 0]
CHUNK_END = [1 + max(s for s in range(LAST) if STEPS[s][:2] == gc) for gc in CHUNKS]


def on_diagonal(s):
    return STEPS[s][2] >= 4 * STEPS[s][1]


def pair_base(p):
    return NS * (p // 2) - (7 if p % 2 == 0 else 1)


def stage_step(p):
    return pair_base(p) - 13


def turn_step(p, i):
    return pair_base(p) - 12 + i


def max_step(p, u):
    return pair_base(p) - 8 + u // 4


def rows_step(p):
    return pair_base(p) - 2


def y_step(n):
    return CHUNK_END[n] + 1


FIRST_STEP = stage_step(0)
FINAL_STEP = y_step(2 * NG - 1)
SHARED = 6


def check_steps(n):
    first = max_step(NP - 1, NU - 1) + 1
    return first + n * (LAST - first) // PIECES


def norm_step(t):
    return (y_step(2 * NG - 2) if t < NT // 2 else FINAL_STEP - NT // 2) + 1 + t

ROUNDS = []
for _s in range(FIRST_STEP, FINAL_STEP + 1):
    ROUNDS += [("turn", p, i) for p in range(NP) for i in range(4) if turn_step(p, i) == _s]
    ROUNDS += [("rows", p, 0) for p in range(NP) if rows_step(p) == _s]
    ROUNDS += [("y", n, 0) for n in range(2 * NG) if y_step(n) == _s]
    if _s == 0:
        EARLY = len(ROUNDS)
ROUND_AT = {r: n for n, r in enumerate(ROUNDS)}

XSTAGE, XTURN, XMAX, XROWS = 9, 8, 7, 6
XLAST = NC * NG
XROUNDS = []
for _s in range(-XSTAGE, XLAST + 2):
    XROUNDS += [("turn", _s + XTURN, i) for i in range(2) if 0 <= _s + XTURN < NP]
    XROUNDS += [("rows", _s + XROWS, 0)] if 0 <= _s + XROWS < NP else []
    XROUNDS += [("y", _s - 2, 0)] if 0 <= _s - 2 < XLAST else []
    if _s == 0:
        XEARLY = len(XROUNDS)
XROUND_AT = {r: n for n, r in enumerate(XROUNDS)}
XUNITS = [(0, 3), (3, 3), (6, 2)]
XSHARED = 3 * XMAX
XNORM = NG + 2
FFN_STEP = XNORM + NT // 2 + 4
FFN_BANKS = 6


def norm_bank(k, what, t):
    if k == 0:
        if t < NT // 2:
            return {"yt": 0, "proj": 1, "xt": 0, "q": 1}[what]
        return {"yt": 0, "proj": 2, "xt": 4, "q": 6}[what] + t % 2
    return {"yt": 0, "proj": 1, "xt": 0}[what] + (6 if t >= NT // 2 else 0)


def norm_stages(k, s):
    first = [XNORM + t if k else norm_step(t) for t in range(NT)]
    lags = {"yt": 0, "proj": 1, "xt": 3} | ({} if k else {"q": 4})
    return [(what, t) for what, lag in lags.items() for t in range(NT) if first[t] + lag == s]


def bank_before(k, what, t):
    uses = [u for s in range(norm_step(NT - 1) + 5) for u in norm_stages(k, s)]
    uses = [u for u in uses[:uses.index((what, t))] if norm_bank(k, *u) == norm_bank(k, what, t)]
    return uses[-1] if uses else None


def decoder_layer(nc, a):
    with ExitStack() as ctx:
        def sb(name, shape, dt):
            return ctx.enter_context(nc.sbuf_tensor(name, shape, dt))

        ffn_w = sb("ffn_w", [P, FO[5]], F32)
        w_qkv = sb("w_qkv", [P, KD, 3 * D], F32)
        w_proj = sb("w_proj", [P, KD, D], F32)
        w_q = sb("w_q", [P, KD, D], F32)
        w_o = sb("w_o", [P, KD, D], F32)
        bias_q = sb("bias_q", [P, D], F32)
        bias_k = sb("bias_k", [P, D], F32)
        bias_v = sb("bias_v", [P, D], F32)
        bias_o = sb("bias_o", [P, D], F32)
        scale_w3 = sb("scale_w3", [P, D], F32)
        scales = sb("scales", [P, 4, KH], F32)
        cos_t = sb("cos_t", [P, NT, DH], F32)
        sin_t = sb("sin_t", [P, NT, DH], F32)
        ident = sb("ident", [P, P], F32)
        ident_bf = sb("ident_bf", [P, P], BF16)
        causal_bf = sb("causal_bf", [P, P], BF16)
        ones = sb("ones", [P, 1], F32)
        minus_half = sb("minus_half", [P, 1], F32)
        xmask_bias = sb("xmask_bias", [P, NT, CP], BF16)
        xmask_t = sb("xmask_t", [P, T], BF16)
        kx_t = sb("kx_t", [P, NP, 2 * CP], F32R)
        vx = sb("vx", [P, VROW], F32)
        tok = sb("tok", [P, NT, D], F32)
        low_bits = sb("low_bits", [P, PW], U32)
        low_max = sb("low_max", [P, 1], F32)
        low_any = sb("low_any", [1, 1], I32)
        max_raw = sb("max_raw", [P, 2, 2, 2, NT], F32)
        max_split = sb("max_split", [P, 2, 2, 2, NT], F32R)
        max_rows = sb("max_rows", [32, 2, P], F32R)
        recip = sb("recip", [P, 16], F32)
        stats = sb("stats", [P, 2, 6], F32)
        mean_var = sb("mean_var", [P, 2, 2], F32)
        var_eps = sb("var_eps", [P, 2, 1], F32)
        rstd = sb("rstd", [P, 2, 1], F32)

        arena = (nc.sbuf_base + 31) // 32 * 32

        def at(name, shape, dt, offset):
            return nc.alloc_sbuf_tensor_at(name, shape, dt, offset=arena + offset)

        O_V, O_QK, O_STAGE, O_T = 0, 9216, 25600, 33792
        O_P = O_T + QKBUF * 8192
        O_Y = O_P + 16384
        v_sb = at("v_sb", [P, NT, VROW], F32, O_V)
        qk_tok = at("qk_tok", [P, 2, NP, NT, 2 * DH], F32, O_QK)
        x_tok = at("x_tok", [P, NT, D], F32, O_T + 3 * 8192)
        stage = [at(f"stage_{n}", [P, NT * 2, 4, DH], F32R, O_STAGE + 4096 * i)
                 for i, n in enumerate("qk")]
        turned = [[at(f"{n}_t{b}", [P, T], F32R, O_T + 8192 * b + 4096 * i) for i, n in enumerate("qk")]
                  for b in range(QKBUF)]
        x_t = at("x_t", [P, KD, T], F32, O_T + 8192 * (QKBUF - 1))
        prob = [at(f"prob{i}", [P, CHUNK], F32, O_P + 2048 * i) for i in range(8)]
        y_sb = at("y_sb", [P, CHUNK], F32, O_Y)
        rope_a = [at(f"rope_a{i}", [P, CHUNK], F32, O_P + 2048 * i) for i in range(2)]
        rope_b = [at(f"rope_b{i}", [P, CHUNK], F32, O_P + 4096 + 2048 * i) for i in range(2)]
        w_kv = at("w_kv", [P, 2, KD, D], F32, O_P + 8192)
        ctx_t = at("ctx_t", [P, KD, CTX], F32, O_P + 12288)
        kx_tok = at("kx_tok", [P, NP, 2, DH], F32, O_P + 13312)
        y_t = [at(f"y_t{i}", [P, KD, P], F32, O_T + 4 * 8192 + 1024 * i) for i in range(2)]
        x1_t = [at(f"x1_t{i}", [P, KD, P], F32, O_T + 4 * 8192 + 2048 + 1024 * i) for i in range(2)]
        resid = [at(f"resid{i}", [P, D], F32, O_T + 4 * 8192 + 4096 + 1024 * i) for i in range(2)]
        qx_t = [at(f"qx_t{i}", [P, T], F32R, O_T + 4096 * i if i < 6 else O_QK + 8192 + 4096 * (i - 6)) for i in range(NP)]
        xmask_u8 = at("xmask_u8", [P, NT, CTX], U8, O_T)
        xmask_t_u8 = at("xmask_t_u8", [CTX, T], U8, O_T + 4096)
        x_hl = [at(f"x_{n}", [P, KD, T], F32R, 8192 * i) for i, n in enumerate(("hi", "lo"))]
        hid = [[at(f"hid{b}_{n}", [P, KH, CHUNK], F32R, 25600 + 32768 * b + 16384 * i)
                for i, n in enumerate(("hi", "lo"))] for b in range(2)]
        act_raw = [at(f"act_raw{i}", [P, CHUNK], F32, 16384 + 2048 * i) for i in range(3)]
        silu_sb = at("silu_sb", [P, CHUNK], F32, 22528)
        resid_f = [at(f"resid_f{i}", [P, D], F32, O_Y + 1024 * i) for i in range(2)]

        bank = [ctx.enter_context(nc.psum_tensor(f"bank{i}", [P, CHUNK], F32)) for i in range(8)]

        def sem(name):
            return ctx.enter_context(nc.semaphore(name))

        w_in, mask_in, ffn_scratch_in, ffn_in = sem("w_in"), sem("mask_in"), sem("ffn_scratch_in"), sem("ffn_in")
        qkv_in = sem("qkv_in")
        set_pool, set_dve = sem("set_pool"), sem("set_dve")
        names = """next_in x_in filled qk_mm v_mm rope_mul rope_add v_evac
            ctx_mm ctx_add ctx_stage ctx_lo ctx_turn ctx_evac
            stage_hi stage_lo round_mm turn_evac rows_evac rows_in0 rows_in1 y_norm
            max_mm max_red max_op score_mm exp_done select_done av_done y_evac
            check_op flag_mm flag_set
            yt_mm yt_evac proj_mm ln_add ln_stats ln_aggr ln_eps ln_rstd ln_done xt_mm xt_evac
            q_mm q_add bo_add x_lo
            xstage_hi xstage_lo xround_mm xturn_evac xrows_evac xrows_in0 xrows_in1 xy_norm
            xmax_mm xmax_red xmax_op xscore_mm xexp_done xmask_dve xmask_pool xav_done xy_evac
            ffn_mm ffn_act ffn_gate act_hi act_lo ffn_out out_done""".split()
        S = {n: sem(n) for n in names}
        first, last = S[names[0]].num, S[names[-1]].num
        assert last - first == len(names) - 1

        def load_sequence(sp, b, arrived):
            sp.dma_start(x_t[:], a["x_t"][bass.ds(b, 1)].rearrange("o (k p) t -> p (o k) t", p=P)).then_inc(arrived, 16)
            sp.dma_start(ctx_t[:], a["ctx_t"][bass.ds(b, 1)].rearrange("o (k p) t -> p (o k) t", p=P)).then_inc(arrived, 16)
            for i, n in enumerate(("w_k", "w_v")):
                sp.dma_start(w_kv[:, i], a[n].rearrange("(k p) n -> p k n", p=P)).then_inc(arrived, 16)

        with nc.Block() as block:
            @block.sync
            def _(sp):
                sp.dma_start(xmask_u8[:], a["mask"].rearrange("(t p) k -> p t k", p=P)).then_inc(mask_in, 16)
                sp.dma_start(xmask_t_u8[:], a["mask_t"]).then_inc(mask_in, 16)
                load_sequence(sp, 0, qkv_in)
                sp.dma_start(w_qkv[:], a["w_qkv"].rearrange("(k p) n -> p k n", p=P)).then_inc(qkv_in, 16)
                sp.dma_start(cos_t[:], a["cos"]).then_inc(qkv_in, 16)
                sp.dma_start(sin_t[:], a["sin"]).then_inc(qkv_in, 16)

            @block.gpsimd
            def _(pool):
                pool.memset(ident[:], 0.0).then_inc(set_pool, 1)
                pool.memset(ident_bf[:], 0.0).then_inc(set_pool, 1)
                pool.memset(causal_bf[:], 0.0).then_inc(set_pool, 1)
                pool.memset(ones[:], 1.0).then_inc(set_pool, 1)
                pool.memset(minus_half[:], -0.5).then_inc(set_pool, 1)
                pool.memset(kx_t[:].bitcast(F32), 0.0).then_inc(set_pool, 1)
                pool.memset(vx[:], 1.0).then_inc(set_pool, 1)
                pool.wait_ge(set_pool, 7)
                for m in (ident, ident_bf):
                    pool.affine_select(out=m[:], in_=m[:], compare_op=ALU.not_equal, fill=1.0, base=0,
                                       pattern=[[-1, P]], channel_multiplier=1).then_inc(set_pool, 1)
                pool.affine_select(out=causal_bf[:], in_=causal_bf[:], compare_op=ALU.is_ge, fill=NEG, base=0,
                                   pattern=[[-1, P]], channel_multiplier=1).then_inc(set_pool, 1)

            @block.vector
            def _(dve):
                dve.memset(xmask_bias[:], 0.0).then_inc(set_dve, 1)
                dve.wait_ge(mask_in, 32)
                dve.wait_ge(set_dve, 1)
                dve.tensor_scalar(xmask_bias[:, :, 0:CTX], xmask_u8[:], 1.0, -NEG, ALU.subtract,
                                  ALU.mult).then_inc(set_dve, 1)
                dve.tensor_copy(xmask_t[0:CTX], xmask_t_u8[:]).then_inc(set_dve, 1)

        with nc.Fori(0, BATCH) as b:
            with nc.Block() as block:
                build_sequence(nc, block, b, dict(locals()), S)
            nc.all_engine_barrier(sems_to_clear=range(first, last + 1))


def build_sequence(nc, block, b, L, S):
    a = L["a"]
    bank, ident, tok, turned, stage, prob = (L[k] for k in ("bank", "ident", "tok", "turned", "stage", "prob"))
    x_t, qk_tok, x_tok, v_sb, y_sb, kx_t, vx = (L[k] for k in ("x_t", "qk_tok", "x_tok", "v_sb", "y_sb", "kx_t", "vx"))
    w_kv, ctx_t, kx_tok = L["w_kv"], L["ctx_t"], L["kx_tok"]
    max_raw, max_split, max_rows, recip = L["max_raw"], L["max_split"], L["max_rows"], L["recip"]
    y_t, x1_t, resid, resid_f, qx_t = L["y_t"], L["x1_t"], L["resid"], L["resid_f"], L["qx_t"]
    x_hl, hid, act_raw, silu_sb, ffn_w, scales = (L[k] for k in ("x_hl", "hid", "act_raw", "silu_sb", "ffn_w", "scales"))
    stats, mean_var, var_eps, rstd = L["stats"], L["mean_var"], L["var_eps"], L["rstd"]
    low_bits, low_max, low_any = L["low_bits"], L["low_max"], L["low_any"]
    qkv_in, w_in, ffn_in, ffn_scratch_in, set_pool, set_dve = (L[k] for k in ("qkv_in", "w_in", "ffn_in", "ffn_scratch_in", "set_pool", "set_dve"))
    A_BANK, S_BANK, Y_BANK, R_BANK = bank[0:2], bank[2:6], bank[6], bank[7]

    def round_bank(n, early):
        return Y_BANK if n < early and n % 2 else R_BANK

    def qkt(p, which):
        return turned[p % QKBUF][which]

    def unit_bank(n):
        return bank[n % SHARED] if n < 2 * NU else A_BANK[n % 2]

    def x_unit_bank(n):
        return bank[n % SHARED] if n < XSHARED else A_BANK[n % 2]

    def v_window(v, h):
        return v[:, VW * h:VW * h + 32]

    def consumer(rounds, n, prefix):
        kind = rounds[n][0]
        count = sum(r[0] == kind for r in rounds[:n + 1])
        name = {"turn": "turn_evac", "rows": "rows_evac", "y": "y_norm"}[kind]
        return S[prefix + name], count * (2 if kind == "y" else 1)

    def w_view(i, dtype):
        n = D if i == 4 else HID
        v = ffn_w[:, FO[i]:FO[i + 1]]
        return (v if dtype is F32 else v.bitcast(dtype)).rearrange("p (k n) -> p k n", n=n)

    @block.sync
    def _(sp):
        with sp.If(b == 0):
            for dst, name in ((L["bias_k"], "bk"), (L["bias_v"], "bv"), (L["bias_q"], "bq"), (L["bias_o"], "bo"), (L["scale_w3"], "s3")):
                sp.dma_start(dst[:], a[name].rearrange("(o n) -> o n", o=1).to_broadcast([P, D])).then_inc(w_in, 16)
            for name in ("w_proj", "w_q", "w_o"):
                sp.dma_start(L[name][:], a[name].rearrange("(k p) n -> p k n", p=P)).then_inc(w_in, 16)
            sp.dma_start(scales[:], a["scales"]).then_inc(w_in, 16)
            for name in ("w1", "w2", "h1", "h2", "w3"):
                sp.dma_start(a["scratch_" + name], a[name]).then_inc(ffn_scratch_in, 16)
            sp.wait_ge(ffn_scratch_in, 16 * 5)
            for i, name in enumerate(("w1", "w2", "h1", "h2", "w3")):
                sp.dma_start(w_view(i, F32), a["scratch_" + name].rearrange("(k p) n -> p k n", p=P)).then_inc(ffn_in, 16)
        for p in range(NP):
            if p == 6:
                sp.wait_ge(S["score_mm"], 4 * NS * 2)
                sp.dma_start(x_tok[:], a["x"][bass.ds(b, 1)].rearrange("o (t p) n -> p (o t) n", p=P)).then_inc(S["x_in"], 16)
            sp.wait_ge(S["rows_evac"], p + 1)
            sp.wait_ge(S["turn_evac"], 4 * p + 4)
            sp.wait_ge(S["max_mm"], NU * (p + 1))
            for hh in range(2):
                for r in range(2):
                    q0 = 16 * hh + 8 * r
                    row = SLOT * hh + MROW + r
                    sp.dma_start(qkt(p, 0)[row:row + 1, :].bitcast(F32), max_rows[q0:q0 + 8, p % 2, :].bitcast(F32)).then_inc(S[f"rows_in{p % 2}"], 16)
        for p in range(NP):
            sp.wait_ge(S["xrows_evac"], p + 1)
            sp.wait_ge(S["xturn_evac"], 2 * p + 2)
            sp.wait_ge(S["xmax_mm"], 3 * (p + 1))
            for hh in range(2):
                for r in range(2):
                    q0 = 16 * hh + 8 * r
                    row = SLOT * hh + MROW + r
                    sp.dma_start(qx_t[p][row:row + 1, :].bitcast(F32), max_rows[q0:q0 + 8, p % 2, :].bitcast(F32)).then_inc(S[f"xrows_in{p % 2}"], 16)
        with sp.If(b < BATCH - 1):
            sp.wait_ge(S["ffn_mm"], 36 * NC - 4)
            L["load_sequence"](sp, nc.s_assert_within(b + 1, 1, BATCH - 1, skip_runtime_bounds_check_because="the branch is taken below the last sequence alone"), S["next_in"])
            sp.wait_ge(S["next_in"], 16 * 4)
        for t in range(NT):
            sp.wait_ge(S["ln_done"], 2 * NT + t + 1)
            sp.dma_start(a["out"][bass.ds(b, 1)].rearrange("o (t p) n -> p (o t) n", p=P)[:, t, :], tok[:, t, :]
                         ).then_inc(S["out_done"], 16)
        sp.wait_ge(S["out_done"], 16 * NT)

    @block.tensor
    def _(pe):
        mm = pe.matmul

        def project_qkv(t):
            if t >= 2:
                pe.wait_ge(S["rope_mul"], 3 * (t - 1))
                pe.wait_ge(S["v_evac"], t - 1)
            qk, v = bank[2 + t % 2], bank[4 + t % 2]
            xs = x_t[:, :, P * t:P * (t + 1)]
            for k in range(KD):
                i = mm(qk[:], xs[:, k], L["w_qkv"][:, k, 0:2 * D], start=k == 0, stop=k == KD - 1)
            i.then_inc(S["qk_mm"], 1)
            for k in range(KD):
                i = mm(v[:, 0:D], xs[:, k], L["w_qkv"][:, k, 2 * D:3 * D], start=k == 0, stop=k == KD - 1)
            i.then_inc(S["v_mm"], 1)

        def project_ctx():
            for i in range(2):
                for k in range(KD):
                    m = mm(bank[i][0:CTX, 0:D], ctx_t[:, k], w_kv[:, i, k], start=k == 0, stop=k == KD - 1)
                m.then_inc(S["ctx_mm"], 1)

        def turn_ctx(j):
            if j == 0:
                pe.wait_ge(S["ctx_stage"], 3)
            for q in range(4):
                m = pe.transpose(bank[j][:, P * q:P * q + CTX], ctx_pair(4 * j + q), ident[0:CTX, 0:CTX])
            m.then_inc(S["ctx_turn"], 1)

        def ctx_pair(p):
            return stage[1][0:CTX, 2 * p:2 * p + 2].rearrange("p h a e -> p (h a e)").bitcast(F32)

        def use_round(rounds, at, key, prefix):
            n, early = at[key], XEARLY if prefix else EARLY
            if n >= 1 and n >= early:
                pe.wait_ge(*consumer(rounds, n - 1, prefix))
            if 2 <= n <= early:
                pe.wait_ge(*consumer(rounds, n - 2, prefix))
            return round_bank(n, early)

        def values_bank_free(rounds, early, prefix):
            pe.wait_ge(*consumer(rounds, early - 1, prefix))
            pe.wait_ge(*consumer(rounds, early - 2, prefix))

        def turn(p, i):
            if i == 0:
                pe.wait_ge(S["stage_hi"], 2 * (p + 1))
                pe.wait_ge(S["stage_lo"], 2 * (p + 1))
            out = use_round(ROUNDS, ROUND_AT, ("turn", p, i), "")
            st = stage[i // 2][:].bitcast(F32)
            for q in range(4):
                t = 4 * (i % 2) + q
                m = pe.transpose(out[:, P * q:P * (q + 1)], st[:, 2 * t:2 * t + 2].rearrange("p h a e -> p (h a e)"), ident[:])
            m.then_inc(S["round_mm"], 1)

        def max_unit(p, u):
            n = NU * p + u
            if u == 0:
                pe.wait_ge(S["turn_evac"], 4 * (p + 1))
            ahead = SHARED if p < 2 else 2
            if n >= ahead:
                pe.wait_ge(S["max_red"], n - ahead + 1)
            hh, qt, half = UNITS[u]
            k0, k1 = CHUNK * half, min(CHUNK * (half + 1), P * (qt + 1))
            out, r = unit_bank(n), slice(SLOT * hh, SLOT * (hh + 1))
            diagonal = k1 == P * (qt + 1)
            m = mm(out[:, 0:k1 - k0], qkt(p, 0)[r, P * qt:P * (qt + 1)], qkt(p, 1)[r, k0:k1], start=True, stop=not diagonal)
            if diagonal:
                m = mm(out[:, k1 - k0 - P:k1 - k0], L["ident_bf"][:], L["causal_bf"][:], start=False, stop=True)
            m.then_inc(S["max_mm"], 1)

        def rows(p):
            pe.wait_ge(S["max_op"], 3 * (p + 1))
            out = use_round(ROUNDS, ROUND_AT, ("rows", p, 0), "")
            src = max_split[:, p % 2].rearrange("p h r t -> p (h r t)").bitcast(F32)
            pe.transpose(out[0:32, 0:P], src, ident[:]).then_inc(S["round_mm"], 1)

        def y_turn(n):
            pe.wait_ge(S["y_evac"], n + 1)
            use_round(ROUNDS, ROUND_AT, ("y", n, 0), "")
            for i in range(4):
                m = pe.transpose(R_BANK[:, P * i:P * (i + 1)], y_sb[:, P * i:P * (i + 1)], ident[:])
            m.then_inc(S["round_mm"], 1)

        def score(s, j):
            g, c, kb = STEPS[s]
            if s % NS == 0 and j == 0:
                pe.wait_ge(S["rows_in0"], 64 * (g + 1))
                pe.wait_ge(S["rows_in1"], 64 * (g + 1))
            q0 = max(0, kb - 4 * c) * P
            if s:
                pe.wait_ge(S["exp_done"], 4 * (s - 1) + j + 1)
            elif j == 0:
                pe.wait_ge(S["max_red"], 2 * NU)
            p, r = 2 * g + j // 2, slice(SLOT * (j % 2), SLOT * (j % 2 + 1))
            mm(S_BANK[j][:, 0:CHUNK - q0], qkt(p, 1)[r, P * kb:P * (kb + 1)],
               qkt(p, 0)[r, CHUNK * c + q0:CHUNK * (c + 1)], start=True, stop=True).then_inc(S["score_mm"], 1)

        def values(s):
            g, c, kb = STEPS[s]
            pe.wait_ge(S["exp_done"], 4 * s + 4)
            diag = max(0, kb - 4 * c) if kb >= 4 * c else 0
            if on_diagonal(s):
                pe.wait_ge(S["select_done"], 4 * sum(on_diagonal(i) for i in range(s + 1)))
            n = CHUNKS.index((g, c))
            if s == 0:
                values_bank_free(ROUNDS, EARLY, "")
            if kb == 0 and n:
                pe.wait_ge(S["y_evac"], n)
            q0 = diag * P
            for j in range(4):
                m = mm(Y_BANK[32 * j:32 * (j + 1), q0:CHUNK], v_window(v_sb[:, kb], 4 * g + j),
                       prob[4 * (s % 2) + j][:, 0:CHUNK - q0], start=kb == 0, stop=kb == 4 * c + 3)
            m.then_inc(S["av_done"], 1)

        def norm_out(k, what, t):
            before = bank_before(k, what, t)
            if before:
                n = NT * k + before[1] + 1
                pe.wait_ge(S[{"yt": "yt_evac", "proj": "ln_add", "xt": "xt_evac", "q": "q_add"}[before[0]]], n)
                if k and before[0] == "xt":
                    pe.wait_ge(S["x_lo"], before[1] + 1)
            return bank[norm_bank(k, what, t)]

        def y_to_features(k, t):
            if t == 0:
                pe.wait_ge(S["xy_norm" if k else "y_norm"], 8 if k else 14)
                pe.wait_ge(S["xmax_red" if k else "max_red"], (3 if k else NU) * NP)
            if t == NT // 2:
                pe.wait_ge(S["xy_norm" if k else "y_norm"], 16)
                pe.wait_ge(S["xy_evac" if k else "exp_done"], XLAST if k else 4 * LAST)
            out = norm_out(k, "yt", t)
            for i in range(KD):
                m = pe.transpose(out[:, P * i:P * (i + 1)], tok[:, t, P * i:P * (i + 1)], ident[:])
            m.then_inc(S["yt_mm"], 1)

        def project_out(k, t):
            pe.wait_ge(S["yt_evac"], NT * k + t + 1)
            out = norm_out(k, "proj", t)
            for i in range(KD):
                m = mm(out[:, 0:D], y_t[t % 2][:, i], L["w_o" if k else "w_proj"][:, i], start=i == 0, stop=i == KD - 1)
            m.then_inc(S["proj_mm"], 1)

        def x_to_features(k, t):
            pe.wait_ge(S["ln_done"], NT * k + t + 1)
            out = norm_out(k, "xt", t)
            for i in range(KD):
                m = pe.transpose(out[:, P * i:P * (i + 1)], tok[:, t, P * i:P * (i + 1)], ident[:])
            m.then_inc(S["xt_mm"], 1)

        def project_q(t):
            pe.wait_ge(S["xt_evac"], t + 1)
            out = norm_out(0, "q", t)
            if t == NT // 2:
                pe.wait_ge(S["y_evac"], 2 * NG)
            for i in range(KD):
                m = mm(out[:, 0:D], x1_t[t % 2][:, i], L["w_q"][:, i], start=i == 0, stop=i == KD - 1)
            m.then_inc(S["q_mm"], 1)

        def norm_products(k, s, which):
            for what, t in norm_stages(k, s):
                if what == "yt" and what in which:
                    y_to_features(k, t)
                if what == "proj" and what in which:
                    project_out(k, t)
                if what == "xt" and what in which:
                    x_to_features(k, t)
                if what == "q" and what in which:
                    project_q(t)

        def x_turn(p, i):
            if i == 0:
                pe.wait_ge(S["xstage_lo"], p + 1)
                pe.wait_ge(S["xstage_hi"], p + 1)
            out = use_round(XROUNDS, XROUND_AT, ("turn", p, i), "x")
            st = stage[0][:].bitcast(F32)
            for q in range(4):
                t = 4 * i + q
                m = pe.transpose(out[:, P * q:P * (q + 1)], st[:, 2 * t:2 * t + 2].rearrange("p h a e -> p (h a e)"), ident[:])
            m.then_inc(S["xround_mm"], 1)

        def x_max(p, u):
            n = 3 * p + u
            if u == 0:
                pe.wait_ge(S["xturn_evac"], 2 * (p + 1))
            ahead = SHARED if n < XSHARED else 2
            if n >= ahead:
                pe.wait_ge(S["xmax_red"], n - ahead + 1)
            t0, nt = XUNITS[u]
            out = x_unit_bank(n)[:, 0:2 * CP * nt]
            mask = L["xmask_bias"][:, t0:t0 + nt].unsqueeze(2).to_broadcast([P, nt, 2, CP])
            mm(out.rearrange("p (t h k) -> p t h k", h=2, k=CP), L["ident_bf"][:], mask, start=True, stop=False)
            for i in range(nt):
                t = t0 + i
                m = mm(out[:, 2 * CP * i:2 * CP * (i + 1)], qx_t[p][:, P * t:P * (t + 1)], kx_t[:, p], start=False, stop=i == nt - 1)
            m.then_inc(S["xmax_mm"], 1)

        def x_rows(p):
            pe.wait_ge(S["xmax_op"], 2 * (p + 1))
            out = use_round(XROUNDS, XROUND_AT, ("rows", p, 0), "x")
            src = max_split[:, p % 2].rearrange("p h r t -> p (h r t)").bitcast(F32)
            pe.transpose(out[0:32, 0:P], src, ident[:]).then_inc(S["xround_mm"], 1)

        def x_scores(s):
            c, g = divmod(s, NG)
            if c == 0:
                pe.wait_ge(S["xrows_in0"], 64 * (g + 1))
                pe.wait_ge(S["xrows_in1"], 64 * (g + 1))
            if s == 0:
                pe.wait_ge(S["xmax_red"], XSHARED)
            for j in range(4):
                if s:
                    pe.wait_ge(S["xexp_done"], 4 * (s - 1) + j + 1)
                p, hh = 2 * g + j // 2, j % 2
                r = slice(SLOT * hh, SLOT * (hh + 1))
                mm(S_BANK[j][0:CTX, :], kx_t[r, p, CP * hh:CP * hh + CTX],
                   qx_t[p][r, CHUNK * c:CHUNK * (c + 1)], start=True, stop=True).then_inc(S["xscore_mm"], 1)

        def x_values(s):
            g = s % NG
            if s == 0:
                values_bank_free(XROUNDS, XEARLY, "x")
            pe.wait_ge(S["xmask_dve"], 2 * s + 2)
            pe.wait_ge(S["xmask_pool"], 2 * s + 2)
            if s:
                pe.wait_ge(S["xy_evac"], s)
            for j in range(4):
                m = mm(Y_BANK[32 * j:32 * (j + 1), :], v_window(vx[0:CTX], 4 * g + j),
                       prob[4 * (s % 2) + j][0:CTX, :], start=True, stop=True)
            m.then_inc(S["xav_done"], 1)

        def x_y_turn(n):
            pe.wait_ge(S["xy_evac"], n + 1)
            use_round(XROUNDS, XROUND_AT, ("y", n, 0), "x")
            for i in range(4):
                m = pe.transpose(R_BANK[:, P * i:P * (i + 1)], y_sb[:, P * i:P * (i + 1)], ident[:])
            m.then_inc(S["xround_mm"], 1)

        def group_free(c, n):
            q = 36 * c + n - FFN_BANKS
            if q < 0:
                return
            c, n = q // 36, q % 36
            if n < 16 and n % 2 == 0:
                pe.wait_ge(S["ffn_act"], 24 * c + n // 2 + 1)
            elif n < 16:
                pe.wait_ge(S["ffn_gate"], 8 * c + n // 2 + 1)
            elif n < 32:
                pe.wait_ge(S["ffn_act"], 24 * c + n - 16 + 8 + 1)
            else:
                pe.wait_ge(S["ffn_out"], 4 * c + n - 32 + 1)

        def ffn(exact):
            dt = F32R if exact else F32

            def view(ap):
                return ap if exact else ap.bitcast(F32)

            for c in range(NC):
                tokens = slice(CHUNK * c, CHUNK * (c + 1))
                pe.wait_ge(S["xt_evac"], NT + 4 * (c + 1))
                pe.wait_ge(S["x_lo"], 4 * (c + 1))
                for m in range(KH):
                    for i in range(2):
                        n = 2 * m + i
                        group_free(c, n)
                        out = bank[(36 * c + n) % FFN_BANKS]
                        for k in range(KD):
                            for part in range(2):
                                o = mm(out[:], w_view(i, dt)[:, k, P * m:P * (m + 1)], view(x_hl[part][:, k, tokens]),
                                       start=k + part == 0, stop=(k, part) == (KD - 1, 1))
                        o.then_inc(S["ffn_mm"], 1)
                    if c == 0:
                        norm_products(1, FFN_STEP + m, ("yt", "proj", "xt"))
                for layer in range(2):
                    src = hid[layer]
                    for m in range(KH):
                        n = 16 + 8 * layer + m
                        group_free(c, n)
                        out = bank[(36 * c + n) % FFN_BANKS]
                        for k in range(KH):
                            if m == 0:
                                pe.wait_ge(S["act_hi"], 24 * c + 8 * layer + k + 1)
                                pe.wait_ge(S["act_lo"], 24 * c + 8 * layer + k + 1)
                            for part in range(2):
                                o = mm(out[:], w_view(2 + layer, dt)[:, k, P * m:P * (m + 1)], view(src[part][:, k]),
                                       start=k + part == 0, stop=(k, part) == (KH - 1, 1))
                        o.then_inc(S["ffn_mm"], 1)
                for i in range(4):
                    n = 32 + i
                    group_free(c, n)
                    out = bank[(36 * c + n) % FFN_BANKS]
                    for k in range(KH):
                        if i == 0:
                            pe.wait_ge(S["act_hi"], 24 * c + 16 + k + 1)
                            pe.wait_ge(S["act_lo"], 24 * c + 16 + k + 1)
                        for part in range(2):
                            o = mm(out[:, 0:D], view(hid[0][part][:, k, P * i:P * (i + 1)]), w_view(4, dt)[:, k],
                                   start=k + part == 0, stop=(k, part) == (KH - 1, 1))
                    o.then_inc(S["ffn_mm"], 1)

        pe.wait_ge(set_pool, 10)
        pe.wait_ge(set_dve, 3)
        pe.wait_ge(qkv_in, 16 * 7)
        for t in range(NT):
            project_qkv(t)
            if t == 1:
                project_ctx()
            if t == 5:
                turn_ctx(0)
            if t == 6:
                turn_ctx(1)
        pe.wait_ge(S["v_evac"], NT)
        pe.wait_ge(S["rope_mul"], 3 * NT)
        pe.wait_ge(S["ctx_evac"], 4)
        pe.wait_ge(w_in, 16 * 9)
        for s in range(FIRST_STEP, norm_step(NT - 1) + 5):
            units = [(p, u) for p in range(NP) for u in range(NU) if max_step(p, u) == s]
            for j in range(4):
                if 0 <= s < LAST:
                    score(s, j)
                for unit in units[j:j + 1]:
                    max_unit(*unit)
                for kind, i, k in ROUNDS:
                    if kind == "turn" and j == 1 and turn_step(i, k) == s:
                        turn(i, k)
                    if kind == "rows" and j == 1 and rows_step(i) == s:
                        rows(i)
                    if kind == "y" and j == 3 and y_step(i) == s:
                        y_turn(i)
            norm_products(0, s, ("yt", "proj"))
            if 0 <= s - 1 < LAST:
                values(s - 1)
            norm_products(0, s, ("xt", "q"))
        with pe.If(b == 0):
            pe.wait_ge(S["check_op"], PIECES + 3)
            pe.wait_ge(S["q_add"], NT)
            mm(S_BANK[3][0:1, 0:1], low_max[:], L["ones"][:], start=True, stop=True).then_inc(S["flag_mm"], 1)
        pe.wait_ge(S["q_add"], NT)
        for s in range(-XSTAGE, FFN_STEP):
            if s == -XMAX:
                with pe.If(b == 0):
                    pe.wait_ge(S["flag_set"], 1)
            if 0 <= s + XTURN < NP:
                x_turn(s + XTURN, 0)
            if 0 <= s < XLAST:
                x_scores(s)
            if 0 <= s + XTURN < NP:
                x_turn(s + XTURN, 1)
            if 0 <= s + XMAX < NP:
                for u in range(3):
                    x_max(s + XMAX, u)
            if 0 <= s + XROWS < NP:
                x_rows(s + XROWS)
            if 0 <= s - 1 < XLAST:
                x_values(s - 1)
            if 0 <= s - 2 < XLAST:
                x_y_turn(s - 2)
            norm_products(1, s, ("yt", "proj", "xt"))
        pe.wait_ge(ffn_in, 16 * 5)
        with pe.register("low_bits_any") as found:
            pe.reg_load(found, low_any[0:1, 0:1])
            with pe.If_eq(found, 0):
                ffn(exact=True)
            with pe.If_ne(found, 0):
                ffn(exact=False)

    @block.scalar
    def _(act):
        def evac_round(rounds, at, key, prefix, out, name, rows=P, columns=CHUNK):
            act.wait_ge(S[prefix + "round_mm"], at[key] + 1)
            src = round_bank(at[key], XEARLY if prefix else EARLY)[0:rows, 0:columns]
            act.activation(out, src, ACT.Copy).then_inc(S[prefix + name], 1)

        def v_evac(t):
            act.wait_ge(S["v_mm"], t + 1)
            if t == 0:
                act.wait_ge(S["filled"], 3)
            act.activation(v_sb[:, t, 0:H * VW].rearrange("p (h w) -> p h w", w=VW)[:, :, 0:DH],
                           bank[4 + t % 2][:, 0:D].rearrange("p (h e) -> p h e", e=DH), ACT.Copy).then_inc(S["v_evac"], 1)

        def ctx_evac(j):
            act.wait_ge(S["ctx_turn"], j + 1)
            for hh in range(2):
                r = slice(SLOT * hh, SLOT * (hh + 1))
                act.activation(kx_t[r, 4 * j:4 * j + 4, CP * hh:CP * hh + CTX],
                               bank[j][r].rearrange("p (q k) -> p q k", k=P)[:, :, 0:CTX], ACT.Copy).then_inc(S["ctx_evac"], 1)

        def turn_evac(p, i):
            if p >= QKBUF:
                act.wait_ge(S["score_mm"], 4 * NS * ((p - QKBUF) // 2 + 1))
            c = CHUNK * (i % 2)
            evac_round(ROUNDS, ROUND_AT, ("turn", p, i), "", qkt(p, i // 2)[:, c:c + CHUNK], "turn_evac")

        def rows_evac(p):
            if p >= 2:
                act.wait_ge(S[f"rows_in{p % 2}"], 64 * (p // 2))
            evac_round(ROUNDS, ROUND_AT, ("rows", p, 0), "", max_rows[:, p % 2], "rows_evac", 32, P)

        def exps(s, heads):
            g, c, kb = STEPS[s]
            n = CHUNK - max(0, kb - 4 * c) * P
            if s >= 2 and heads[0] == 0:
                act.wait_ge(S["av_done"], s - 1)
            for j in heads:
                act.wait_ge(S["score_mm"], 4 * s + j + 1)
                act.activation(prob[4 * (s % 2) + j][:, 0:n], S_BANK[j][:, 0:n], ACT.Exp, scale=SCALE).then_inc(S["exp_done"], 1)

        def yt_evac(k, t):
            n = NT * k + t
            act.wait_ge(S["yt_mm"], n + 1)
            if n >= 2:
                act.wait_ge(S["proj_mm"], n - 1)
            else:
                act.wait_ge(S["score_mm"], 4 * NS * (NG - 1))
            act.activation(y_t[t % 2][:], bank[norm_bank(k, "yt", t)][:, 0:D].rearrange("p (k n) -> p k n", k=KD), ACT.Copy).then_inc(S["yt_evac"], 1)

        def xt_evac(k, t):
            act.wait_ge(S["xt_mm"], NT * k + t + 1)
            if k == 0 and t >= 2:
                act.wait_ge(S["q_mm"], t - 1)
            out = x_hl[0][:, :, P * t:P * (t + 1)] if k else x1_t[t % 2][:]
            act.activation(out, bank[norm_bank(k, "xt", t)][:, 0:D].rearrange("p (k n) -> p k n", k=KD), ACT.Copy).then_inc(S["xt_evac"], 1)

        def norm_evacs(k, s):
            for what, t in norm_stages(k, s):
                if what == "yt":
                    yt_evac(k, t)
                if what == "xt":
                    xt_evac(k, t)

        def x_exps(s):
            if s >= 2:
                act.wait_ge(S["xav_done"], s - 1)
            for j in range(4):
                act.wait_ge(S["xscore_mm"], 4 * s + j + 1)
                act.activation(prob[4 * (s % 2) + j][0:CTX], S_BANK[j][0:CTX, :], ACT.Exp, scale=SCALE).then_inc(S["xexp_done"], 1)

        act.wait_ge(set_pool, 10)
        for t in range(NT):
            v_evac(t)
            if t == 5:
                ctx_evac(0)
            if t == 6:
                ctx_evac(1)
        act.wait_ge(S["rope_add"], NT)
        for s in range(FIRST_STEP, norm_step(NT - 1) + 5):
            if 0 <= s < LAST:
                exps(s, (0, 1))
            for kind, i, j in ROUNDS:
                if kind == "turn" and turn_step(i, j) == s:
                    turn_evac(i, j)
                if kind == "rows" and rows_step(i) == s:
                    rows_evac(i)
            if 0 <= s < LAST:
                exps(s, (2, 3))
            norm_evacs(0, s)
        act.wait_ge(S["q_mm"], NT)
        act.wait_ge(S["ln_done"], NT)
        for s in range(-XSTAGE, FFN_STEP):
            if 0 <= s + XTURN < NP:
                evac_round(XROUNDS, XROUND_AT, ("turn", s + XTURN, 0), "x", qx_t[s + XTURN][:, 0:CHUNK], "turn_evac")
            if 0 <= s < XLAST:
                x_exps(s)
            if 0 <= s + XTURN < NP:
                evac_round(XROUNDS, XROUND_AT, ("turn", s + XTURN, 1), "x", qx_t[s + XTURN][:, CHUNK:T], "turn_evac")
            if 0 <= s + XROWS < NP:
                p = s + XROWS
                if p >= 2:
                    act.wait_ge(S[f"xrows_in{p % 2}"], 64 * (p // 2))
                else:
                    act.wait_ge(S[f"rows_in{p % 2}"], 64 * NG)
                evac_round(XROUNDS, XROUND_AT, ("rows", p, 0), "x", max_rows[:, p % 2], "rows_evac", 32, P)
            if s == XNORM:
                act.wait_ge(S["xstage_lo"], NP)
                act.wait_ge(S["xstage_hi"], NP)
            norm_evacs(1, s)
        for c in range(NC):
            for m in range(KH):
                act.wait_ge(S["ffn_mm"], 36 * c + 2 * m + 1)
                if c or m:
                    act.wait_ge(S["ffn_gate"], 8 * c + m)
                act.activation(silu_sb[:], bank[(36 * c + 2 * m) % FFN_BANKS][:], ACT.Silu, scale=scales[:, 0, m:m + 1]).then_inc(S["ffn_act"], 1)
                if c == 0:
                    norm_evacs(1, FFN_STEP + m)
            for layer in range(2):
                for m in range(KH):
                    r = 24 * c + 8 + 8 * layer + m
                    n = 36 * c + 16 + 8 * layer + m
                    act.wait_ge(S["ffn_mm"], n + 1)
                    act.wait_ge(S["act_hi"], r - 2)
                    act.wait_ge(S["act_lo"], r - 2)
                    act.activation(act_raw[r % 3][:], bank[n % FFN_BANKS][:], ACT.Gelu, scale=scales[:, 2 + layer, m:m + 1]).then_inc(S["ffn_act"], 1)

    @block.vector
    def _(dve):
        tt = dve.tensor_tensor

        def rope(t):
            dve.wait_ge(S["qk_mm"], t + 1)
            if t >= 2:
                dve.wait_ge(S["rope_add"], t - 1)
            x = bank[2 + t % 2][:].rearrange("p (h e) -> p h e", e=DH)
            ra, rb = (r[t % 2][:].rearrange("p (h e) -> p h e", e=DH) for r in (L["rope_a"], L["rope_b"]))
            cos, sin = (L[n][:, t].unsqueeze(1).to_broadcast([P, 2 * H, DH]) for n in ("cos_t", "sin_t"))
            h = DH // 2
            tt(ra, x, cos, ALU.mult).then_inc(S["rope_mul"], 1)
            tt(rb[:, :, 0:h], x[:, :, h:DH], sin[:, :, 0:h], ALU.mult).then_inc(S["rope_mul"], 1)
            tt(rb[:, :, h:DH], x[:, :, 0:h], sin[:, :, h:DH], ALU.mult).then_inc(S["rope_mul"], 1)

        def ctx_add():
            dve.wait_ge(S["ctx_mm"], 1)
            tt(kx_tok[0:CTX].rearrange("p a h e -> p (a h e)"), bank[0][0:CTX, 0:D], L["bias_k"][0:CTX], ALU.add).then_inc(S["ctx_add"], 1)
            dve.wait_ge(S["ctx_mm"], 2)
            tt(vx[0:CTX, 0:H * VW].rearrange("p (h w) -> p h w", w=VW)[:, :, 0:DH],
               bank[1][0:CTX, 0:D].rearrange("p (h e) -> p h e", e=DH),
               L["bias_v"][0:CTX].rearrange("p (h e) -> p h e", e=DH), ALU.add).then_inc(S["ctx_add"], 1)
            dve.wait_ge(S["ctx_add"], 1)
            dve.wait_ge(S["filled"], 3)
            k = kx_tok[0:CTX].rearrange("p a h e -> p (a h) e")
            st = stage[1][0:CTX]
            for i, part in enumerate((0, 2)):
                dve.tensor_copy(st[:, :, part], k).then_inc(S["ctx_stage"], 1)
            dve.wait_ge(S["ctx_stage"], 2)
            tt(st[:, :, 1], k, st[:, :, 0].bitcast(F32), ALU.subtract).then_inc(S["ctx_stage"], 1)

        def stage_hi(p):
            if p == 0:
                dve.wait_ge(S["rope_add"], NT)
                dve.wait_ge(S["ctx_turn"], 2)
                dve.wait_ge(S["filled"], 3)
            else:
                dve.wait_ge(S["round_mm"], ROUND_AT[("turn", p - 1, 3)] + 1)
            for i in range(2):
                src = qk_tok[:, i, p].rearrange("p t (h e) -> p (t h) e", h=2).unsqueeze(2).to_broadcast([P, 2 * NT, 2, DH])
                dst = stage[i][:, :, 0:3 if i else 2:2 if i else 1]
                dve.tensor_copy(dst, src).then_inc(S["stage_hi"], 1)
            for i in range(2) if p == 0 else ():
                dve.wait_ge(S["stage_hi"], i + 1)
                src = qk_tok[:, i, p].rearrange("p t (h e) -> p (t h) e", h=2)
                tt(stage[i][:, :, 1 if i else 2], src, stage[i][:, :, 0].bitcast(F32), ALU.subtract).then_inc(S["stage_lo"], 1)

        def reduce_unit(p, u):
            n = NU * p + u
            hh, qt, half = UNITS[u]
            if u == 0 and p >= 2:
                dve.wait_ge(S["max_op"], 3 * (p - 1))
            dve.wait_ge(S["max_mm"], n + 1)
            k = min(CHUNK, P * (qt + 1) - CHUNK * half)
            dve.tensor_reduce(max_raw[:, p % 2, hh, half, qt:qt + 1], unit_bank(n)[:, 0:k], AXX, ALU.max).then_inc(S["max_red"], 1)

        def split_max(p):
            raw, sp = max_raw[:, p % 2], max_split[:, p % 2]
            dve.wait_ge(S["max_red"], NU * (p + 1))
            tt(raw[:, :, 0, 4:NT], raw[:, :, 0, 4:NT], raw[:, :, 1, 4:NT], ALU.max).then_inc(S["max_op"], 1)
            dve.wait_ge(S["max_op"], 3 * p + 1)
            if p >= 2:
                dve.wait_ge(S["round_mm"], ROUND_AT[("rows", p - 2, 0)] + 1)
            dve.tensor_scalar(sp[:, :, 0], raw[:, :, 0], -1.0, None, ALU.mult).then_inc(S["max_op"], 1)
            dve.wait_ge(S["max_op"], 3 * p + 2)
            dve.scalar_tensor_tensor(out=sp[:, :, 1], in0=raw[:, :, 0], scalar=-1.0, in1=sp[:, :, 0].bitcast(F32),
                                     op0=ALU.mult, op1=ALU.subtract).then_inc(S["max_op"], 1)

        def y_evac(n, x=""):
            if n:
                at, rounds = (XROUND_AT, "xround_mm") if x else (ROUND_AT, "round_mm")
                dve.wait_ge(S[rounds], at[("y", n - 1, 0)] + 1)
            dve.wait_ge(S[x + "av_done"], n + 1 if x else CHUNK_END[n])
            dve.tensor_copy(y_sb[:], Y_BANK[:]).then_inc(S[x + "y_evac"], 1)

        def y_norm(n, x=""):
            at = XROUND_AT if x else ROUND_AT
            dve.wait_ge(S[x + "round_mm"], at[("y", n, 0)] + 1)
            g, c = (n % NG, n // NG) if x else CHUNKS[n]
            y = R_BANK[:].rearrange("p (i j e) -> p i j e", i=4, j=4)
            rc = recip[:].rearrange("p (i j o) -> p i j o", i=4, j=4)
            if n:
                dve.wait_ge(S[x + "y_norm"], 2 * n)
            dve.reciprocal(rc, y[:, :, :, DH:DH + 1]).then_inc(S[x + "y_norm"], 1)
            dve.wait_ge(S[x + "y_norm"], 2 * n + 1)
            out = tok[:, 4 * c:4 * c + 4, 4 * DH * g:4 * DH * (g + 1)].rearrange("p i (j e) -> p i j e", e=DH)
            tt(out, y[:, :, :, 0:DH], rc.to_broadcast([P, 4, 4, DH]), ALU.mult).then_inc(S[x + "y_norm"], 1)

        def check_piece(n):
            with dve.If(b == 0):
              if n == 0:
                dve.wait_ge(ffn_in, 16 * 5)
              dve.wait_ge(S["check_op"], n + 1)
              tt(low_bits[:], low_bits[:], ffn_w[:, PW * n:PW * (n + 1)].bitcast(U32), ALU.bitwise_or).then_inc(S["check_op"], 1)

        def ln_stats(n, xr):
            dve.wait_ge(S["ln_add"], n + 1)
            dve.bn_stats(stats[:, n % 2], xr).then_inc(S["ln_stats"], 1)
            dve.wait_ge(S["ln_stats"], n + 1)
            dve.bn_aggr(mean_var[:, n % 2], stats[:, n % 2]).then_inc(S["ln_aggr"], 1)

        def ln_finish(n, xr):
            dve.wait_ge(S["ln_rstd"], n + 1)
            dve.wait_ge(S["ln_aggr"], n + 1)
            dve.tensor_scalar(tok[:, n % NT], xr, mean_var[:, n % 2, 0:1], rstd[:, n % 2], ALU.subtract, ALU.mult).then_inc(S["ln_done"], 1)

        def residual(k, t):
            n = NT * k + t
            dve.wait_ge(S["proj_mm"], n + 1)
            if n >= 2:
                dve.wait_ge(S["ln_done"], n - 1)
            dve.wait_ge(S["bo_add"] if k else S["x_in"], t + 1 if k else 16)
            tt(resid[t % 2][:], bank[norm_bank(k, "proj", t)][:, 0:D], x_tok[:, t], ALU.add).then_inc(S["ln_add"], 1)
            ln_stats(n, resid[t % 2][:])

        def q_add(t):
            dve.wait_ge(S["q_mm"], t + 1)
            tt(qk_tok[:, 0, :, t], bank[norm_bank(0, "q", t)][:, 0:D].rearrange("p (a e) -> p a e", a=NP),
               L["bias_q"][:].rearrange("p (a e) -> p a e", a=NP), ALU.add).then_inc(S["q_add"], 1)

        def x_stage_hi(p):
            if p:
                dve.wait_ge(S["xround_mm"], XROUND_AT[("turn", p - 1, 1)] + 1)
            else:
                dve.wait_ge(S["q_add"], NT)
            src = qk_tok[:, 0, p].rearrange("p t (h e) -> p (t h) e", h=2).unsqueeze(2).to_broadcast([P, 2 * NT, 2, DH])
            dve.tensor_copy(stage[0][:, :, 0:2], src).then_inc(S["xstage_hi"], 1)
            if p == 0:
                dve.wait_ge(S["xstage_hi"], 1)
                src = qk_tok[:, 0, p].rearrange("p t (h e) -> p (t h) e", h=2)
                tt(stage[0][:, :, 2], src, stage[0][:, :, 0].bitcast(F32), ALU.subtract).then_inc(S["xstage_lo"], 1)

        def x_reduce(p, u):
            n = 3 * p + u
            if u == 0:
                if p >= 2:
                    dve.wait_ge(S["xmax_op"], 2 * (p - 1))
            dve.wait_ge(S["xmax_mm"], n + 1)
            t0, nt = XUNITS[u]
            src = x_unit_bank(n)[:, 0:2 * CP * nt].rearrange("p (t h k) -> p t h k", h=2, k=CP)[:, :, :, 0:CTX]
            dst = max_raw[:, p % 2, :, 0, t0:t0 + nt].rearrange("p h t -> p t h")
            dve.tensor_reduce(dst, src, AXX, ALU.max).then_inc(S["xmax_red"], 1)

        def x_split_max(p):
            raw, sp = max_raw[:, p % 2], max_split[:, p % 2]
            dve.wait_ge(S["xmax_red"], 3 * (p + 1))
            if p >= 2:
                dve.wait_ge(S["xround_mm"], XROUND_AT[("rows", p - 2, 0)] + 1)
            dve.tensor_scalar(sp[:, :, 0], raw[:, :, 0], -1.0, None, ALU.mult).then_inc(S["xmax_op"], 1)
            dve.wait_ge(S["xmax_op"], 2 * p + 1)
            dve.scalar_tensor_tensor(out=sp[:, :, 1], in0=raw[:, :, 0], scalar=-1.0, in1=sp[:, :, 0].bitcast(F32),
                                     op0=ALU.mult, op1=ALU.subtract).then_inc(S["xmax_op"], 1)

        def x_mask(s):
            for j in range(2):
                dve.wait_ge(S["xexp_done"], 4 * s + j + 1)
                pr = prob[4 * (s % 2) + j][0:CTX]
                tt(pr, pr, L["xmask_t"][0:CTX, CHUNK * (s // NG):CHUNK * (s // NG + 1)], ALU.mult).then_inc(S["xmask_dve"], 1)

        def input_lo(t):
            dve.wait_ge(S["xt_evac"], NT + t + 1)
            sl = slice(P * t, P * (t + 1))
            tt(x_hl[1][:, :, sl], bank[norm_bank(1, "xt", t)][:, 0:D].rearrange("p (k n) -> p k n", k=KD),
               x_hl[0][:, :, sl].bitcast(F32), ALU.subtract).then_inc(S["x_lo"], 1)

        def norm_work(k, s):
            for what, t in norm_stages(k, s):
                if what == "proj":
                    residual(k, t)
            for what, t in norm_stages(k, s - 1):
                if what == "proj":
                    ln_finish(NT * k + t, resid[t % 2][:])
            for what, t in norm_stages(k, s):
                if what == "q":
                    q_add(t)
                if what == "xt" and k:
                    input_lo(t)

        def hi_part(r, dst):
            dve.tensor_copy(dst, act_raw[r % 3][:]).then_inc(S["act_hi"], 1)

        dve.wait_ge(qkv_in, 16 * 7)
        dve.wait_ge(set_pool, 10)
        for t in range(NT):
            rope(t)
            if t == 2:
                dve.wait_ge(w_in, 16 * 9)
                ctx_add()
        for s in range(FIRST_STEP, norm_step(NT - 1) + 5):
            for p in range(NP):
                if stage_step(p) == s:
                    stage_hi(p)
            for p in range(NP):
                for u in range(NU):
                    if max_step(p, u) == s:
                        reduce_unit(p, u)
                if max_step(p, NU - 1) == s:
                    split_max(p)
            for n in range(PIECES):
                if check_steps(n) == s:
                    check_piece(n)
            for n in range(2 * NG):
                if y_step(n) == s:
                    y_norm(n)
                if CHUNK_END[n] == s:
                    y_evac(n)
            if s == LAST:
                with dve.If(b == 0):
                    dve.wait_ge(S["check_op"], PIECES + 1)
                    dve.tensor_scalar(low_bits[:], low_bits[:], LOWBITS, None, ALU.bitwise_and).then_inc(S["check_op"], 1)
                    dve.wait_ge(S["check_op"], PIECES + 2)
                    dve.tensor_reduce(low_max[:], low_bits[:], AXX, ALU.max).then_inc(S["check_op"], 1)
            norm_work(0, s)
        with dve.If(b == 0):
            dve.wait_ge(S["flag_mm"], 1)
            dve.tensor_copy(low_any[:], S_BANK[3][0:1, 0:1]).then_inc(S["flag_set"], 1)
        for s in range(-XSTAGE, FFN_STEP):
            if 0 <= s + XSTAGE < NP:
                x_stage_hi(s + XSTAGE)
            if 0 <= s + XMAX < NP:
                for u in range(3):
                    x_reduce(s + XMAX, u)
                x_split_max(s + XMAX)
            if 0 <= s < XLAST:
                x_mask(s)
            if 0 <= s - 1 < XLAST:
                y_evac(s - 1, "x")
            if 0 <= s - 2 < XLAST:
                y_norm(s - 2, "x")
            norm_work(1, s)
        for c in range(NC):
            for m in range(KH):
                r, n = 24 * c + m, 36 * c + 2 * m + 1
                dve.wait_ge(S["ffn_mm"], n + 1)
                dve.wait_ge(S["ffn_act"], 24 * c + m + 1)
                if r >= 3:
                    dve.wait_ge(S["act_hi"], r - 2)
                    dve.wait_ge(S["act_lo"], r - 2)
                dve.scalar_tensor_tensor(out=act_raw[r % 3][:], in0=bank[n % FFN_BANKS][:], scalar=scales[:, 1, m:m + 1],
                                         in1=silu_sb[:], op0=ALU.mult, op1=ALU.mult).then_inc(S["ffn_gate"], 1)
                dve.wait_ge(S["ffn_gate"], 8 * c + m + 1)
                hi_part(r, hid[0][0][:, m])
                if c == 0:
                    norm_work(1, FFN_STEP + m)
            for layer in range(2):
                for m in range(KH):
                    r = 24 * c + 8 + 8 * layer + m
                    dve.wait_ge(S["ffn_act"], r + 1)
                    hi_part(r, hid[1 - layer][0][:, m])
            for i in range(5):
                if i < 4:
                    t = 4 * c + i
                    n = 2 * NT + t
                    xr = resid_f[t % 2]
                    dve.wait_ge(S["ffn_mm"], 36 * c + 32 + i + 1)
                    if t >= 2:
                        dve.wait_ge(S["ln_done"], n - 1)
                    tt(xr[:], bank[(36 * c + 32 + i) % FFN_BANKS][:, 0:D], L["scale_w3"][:], ALU.mult).then_inc(S["ffn_out"], 1)
                    dve.wait_ge(S["ffn_out"], t + 1)
                    tt(xr[:], xr[:], tok[:, t], ALU.add).then_inc(S["ln_add"], 1)
                    ln_stats(n, xr[:])
                if i >= 1:
                    t = 4 * c + i - 1
                    ln_finish(2 * NT + t, resid_f[t % 2][:])

    @block.gpsimd
    def _(pool):
        pt = pool.tensor_tensor
        pool.memset(v_sb[:], 1.0).then_inc(S["filled"], 1)
        pool.memset(stage[0][:, :, 3].bitcast(F32), 0.0).then_inc(S["filled"], 1)
        pool.memset(stage[1][:, :, 3].bitcast(F32), 1.0).then_inc(S["filled"], 1)
        pool.memset(low_bits[:], 0).then_inc(S["check_op"], 1)

        def rope_add(t):
            pool.wait_ge(S["rope_mul"], 3 * (t + 1))
            out = qk_tok[:, :, :, t].rearrange("p a b e -> p (a b) e")
            ra, rb = (r[t % 2][:].rearrange("p (a e) -> p a e", a=2 * NP) for r in (L["rope_a"], L["rope_b"]))
            pt(out, ra, rb, ALU.add).then_inc(S["rope_add"], 1)

        def stage_lo(p):
            for i in range(2):
                pool.wait_ge(S["stage_hi"], 2 * p + i + 1)
                src = qk_tok[:, i, p].rearrange("p t (h e) -> p (t h) e", h=2)
                pt(stage[i][:, :, 1 if i else 2], src, stage[i][:, :, 0].bitcast(F32), ALU.subtract).then_inc(S["stage_lo"], 1)

        def select(s):
            if not on_diagonal(s):
                return
            for j in range(4):
                pool.wait_ge(S["exp_done"], 4 * s + j + 1)
                pr = prob[4 * (s % 2) + j][:, 0:P]
                pool.affine_select(out=pr, in_=pr, compare_op=ALU.is_ge, fill=0.0, base=0,
                                   pattern=[[1, P]], channel_multiplier=-1).then_inc(S["select_done"], 1)

        def ln_rstd(n):
            pool.wait_ge(S["ln_aggr"], n + 1)
            if n >= 2:
                pool.wait_ge(S["ln_done"], n - 1)
            pool.tensor_scalar(var_eps[:, n % 2], mean_var[:, n % 2, 1:2], EPS, None, ALU.add).then_inc(S["ln_eps"], 1)
            pool.wait_ge(S["ln_eps"], n + 1)
            pt(rstd[:, n % 2], var_eps[:, n % 2], L["minus_half"][:], ALU.pow).then_inc(S["ln_rstd"], 1)

        for t in range(NT):
            rope_add(t)
        pool.wait_ge(w_in, 16 * 9)
        for s in range(FIRST_STEP, norm_step(NT - 1) + 5):
            for p in range(1, NP):
                if stage_step(p) == s:
                    stage_lo(p)
            if 0 <= s < LAST:
                select(s)
            for t in range(NT):
                if norm_step(t) + 1 == s:
                    ln_rstd(t)
            for t in range(NT):
                if norm_step(t) + 2 == s:
                    pool.wait_ge(S["ln_done"], t + 1)
                    pt(x_tok[:, t], tok[:, t], L["bias_o"][:], ALU.add).then_inc(S["bo_add"], 1)
        for s in range(-XSTAGE, FFN_STEP):
            if 1 <= s + XSTAGE < NP:
                p = s + XSTAGE
                pool.wait_ge(S["xstage_hi"], p + 1)
                src = qk_tok[:, 0, p].rearrange("p t (h e) -> p (t h) e", h=2)
                pt(stage[0][:, :, 2], src, stage[0][:, :, 0].bitcast(F32), ALU.subtract).then_inc(S["xstage_lo"], 1)
            if 0 <= s < XLAST:
                for j in range(2, 4):
                    pool.wait_ge(S["xexp_done"], 4 * s + j + 1)
                    pr = prob[4 * (s % 2) + j][0:CTX]
                    pt(pr, pr, L["xmask_t"][0:CTX, CHUNK * (s // NG):CHUNK * (s // NG + 1)], ALU.mult).then_inc(S["xmask_pool"], 1)
            if 0 <= s - XNORM - 1 < NT:
                ln_rstd(NT + s - XNORM - 1)
        for c in range(NC):
            for r in range(24):
                n = 24 * c + r
                dst = hid[0 if r < 8 or r >= 16 else 1]
                pool.wait_ge(S["act_hi"], n + 1)
                pt(dst[1][:, r % 8], act_raw[n % 3][:], dst[0][:, r % 8].bitcast(F32), ALU.subtract).then_inc(S["act_lo"], 1)
                if c == 0 and FFN_STEP + r - XNORM - 1 < NT:
                    ln_rstd(NT + FFN_STEP + r - XNORM - 1)
            for i in range(4):
                ln_rstd(2 * NT + 4 * c + i)


def rope_tables():
    half = DH // 2
    theta = (np.float32(1.0) / np.float32(10000.0) ** (np.arange(half, dtype=np.float32) / np.float32(half))).astype(np.float32)
    freqs = (np.arange(T, dtype=np.float32)[:, None] * theta[None, :]).astype(np.float32)
    cos = np.repeat(np.cos(freqs), 2, axis=-1).astype(np.float32)
    sin = np.repeat(np.sin(freqs), 2, axis=-1).astype(np.float32)
    sin[:, :half] *= -1
    return [np.ascontiguousarray(t.reshape(NT, P, DH).transpose(1, 0, 2)) for t in (cos, sin)]


def kernel(**inputs):
    import concourse.bacc as bacc
    from concourse.bass_utils import run_bass_kernel_spmd

    g = {k: np.asarray(v) for k, v in inputs.items()}
    cos, sin = rope_tables()
    mask = g["mask_SxS2_bf1"].view(np.uint8)
    arrays = {
        "x": g["x"], "x_t": g["x"].transpose(0, 2, 1), "ctx_t": g["ctx_1024"].transpose(0, 2, 1),
        "mask": mask, "mask_t": mask.T,
        "w_qkv": g["L0_attn_w_qkv"], "w_proj": g["L0_attn_w_proj"],
        "w_q": g["L0_xattn_Wq"].T, "w_k": g["L0_xattn_Wk"].T, "w_v": g["L0_xattn_Wv"].T, "w_o": g["L0_xattn_Wo"].T,
        "bq": g["L0_xattn_bq"], "bk": g["L0_xattn_bk"], "bv": g["L0_xattn_bv"], "bo": g["L0_xattn_bo"],
        "w1": g["L0_ffn_w1_w"].T, "w2": g["L0_ffn_w2_w"].T, "h1": g["L0_ffn_h1_w"].T, "h2": g["L0_ffn_h2_w"].T,
        "w3": g["L0_ffn_w3_w"].T, "s3": g["L0_ffn_w3_s"],
        "scales": np.stack([g[f"L0_ffn_{n}_s"].reshape(KH, P).T for n in ("w1", "w2", "h1", "h2")], axis=1),
        "cos": cos, "sin": sin,
    }
    nc = bacc.Bacc("TRN2", target_bir_lowering=False, num_devices=1, dynamic_dma_scratch_size=1024)
    aps, feeds = {}, {}
    for name, arr in arrays.items():
        arr = np.ascontiguousarray(arr)
        feeds["in_" + name] = arr
        aps[name] = nc.dram_tensor("in_" + name, arr.shape, mybir.dt.from_np(arr.dtype), kind="ExternalInput").ap()
    for name in ("w1", "w2", "h1", "h2", "w3"):
        aps["scratch_" + name] = nc.dram_tensor("scratch_" + name, arrays[name].shape, F32).ap()
    aps["out"] = nc.dram_tensor("out_0", (BATCH, T, D), F32, kind="ExternalOutput").ap()
    decoder_layer(nc, aps)
    r = run_bass_kernel_spmd(nc, [feeds], core_ids=[0])
    return r.results[0]["out_0"]
```
